# Optimizing a Trainium2 kernel written in Bass

```python
import numpy as np
import jax
import jax.numpy as jnp

def _softmax(x, axis=-1):
    return jax.nn.softmax(x, axis=axis)

def _gelu(x):
    return jax.nn.gelu(x, approximate=True)

def _silu(x):
    return jax.nn.silu(x)

def _sigmoid(x):
    return jax.nn.sigmoid(x)

def _layernorm(x, axis=-1, eps=1e-05):
    m = jnp.mean(x, axis=axis, keepdims=True)
    v = jnp.var(x, axis=axis, keepdims=True)
    return (x - m) / jnp.sqrt(v + eps)

def _scatter_add(tgt, idx, src, axis=0):
    return tgt.at[idx].add(src)

def _segment_sum(src, seg, n):
    return jax.ops.segment_sum(src, seg, n)
kernel_name = 'mk_xattn_ffn_d4_seqx_r8_ae9cbb'

def setup_inputs(seed: int=0):
    np.random.seed(seed)
    _w = jnp.asarray

    def _rec_inputs():
        import jax
        import jax.numpy as jnp
        _rk = jax.random.key(seed)
        x = -0.000125 + 0.9999 * jax.random.normal(jax.random.fold_in(_rk, 1), (4, 256, 256), jnp.float32)
        _lenS = 256 - jax.random.randint(jax.random.fold_in(_rk, 7), (4,), 0, max(1, 256 // 4) + 1, jnp.int32)
        _lenS2 = 256 - jax.random.randint(jax.random.fold_in(_rk, 8), (4,), 0, max(1, 256 // 4) + 1, jnp.int32)
        fside_BxS2xS2_0 = -3.05549e-07 + 0.0199987 * jax.random.normal(jax.random.fold_in(_rk, 11), (4, 256, 256), jnp.float32)
        _ctx_1024P = jax.random.normal(jax.random.fold_in(_rk, 12), (4, 16, 128), jnp.float32)
        _ctx_1024c = jax.random.dirichlet(jax.random.fold_in(_rk, 512), 0.3 * jnp.ones((16,), jnp.float32), (4, 256))
        _ctx_1024t = jnp.einsum('bsk,bkd->bsd', _ctx_1024c, _ctx_1024P)
        _ctx_1024t = _ctx_1024t * jax.lax.rsqrt(jnp.mean(jnp.square(_ctx_1024t)) + 1e-12) * 0.953939
        ctx_1024 = 6.82029e-06 + 0.0200006 * (_ctx_1024t + 0.3 * jax.random.normal(jax.random.fold_in(_rk, 612), (4, 256, 128), jnp.float32))
        return (x, fside_BxS2xS2_0, ctx_1024)
    x, fside_BxS2xS2_0, ctx_1024 = _rec_inputs()

    def _L0_xattn_setup():
        import jax, jax.numpy as jnp
        import numpy as np
        EPS = 1e-06
        QMAX = 127.0

        def _smooth_quant_linear(x, w):
            amax_x = jnp.max(jnp.abs(x), axis=0)
            amax_w = jnp.max(jnp.abs(w), axis=0)
            s = jnp.sqrt(jnp.maximum(amax_x, EPS) / jnp.maximum(amax_w, EPS))
            s = jnp.maximum(s, EPS)
            xs = x / s
            ws = w * s
            x_scale = jnp.maximum(jnp.max(jnp.abs(xs), axis=-1, keepdims=True), EPS) / QMAX
            w_scale = jnp.maximum(jnp.max(jnp.abs(ws), axis=-1, keepdims=True), EPS) / QMAX
            x_q = jnp.clip(jnp.round(xs / x_scale), -QMAX, QMAX)
            w_q = jnp.clip(jnp.round(ws / w_scale), -QMAX, QMAX)
            return x_q @ w_q.T * x_scale * w_scale.T

        def _expert_forward(xe, guw, dw):
            h = _smooth_quant_linear(xe, guw)
            gate, up = jnp.split(h, 2, axis=-1)
            a = jax.nn.silu(gate) * up
            return _smooth_quant_linear(a, dw)
        key = jax.random.key(seed)
        k1, k2, k3 = jax.random.split(key, 3)
        E, T, D, I = (8, 256, 256, 128)
        x = jax.random.normal(k1, (E, T, D), dtype=jnp.float32)
        gate_up_weight = jax.random.normal(k2, (E, 2 * I, D), dtype=jnp.float32) * 0.02
        down_weight = jax.random.normal(k3, (E, D, I), dtype=jnp.float32) * 0.02
        return {'x': x, 'gate_up_weight': gate_up_weight, 'down_weight': down_weight}
    _L0_xattn_all = _L0_xattn_setup()
    _L0_xattn_in = {k: v for k, v in _L0_xattn_all.items() if k in ()}
    del _L0_xattn_all

    def _L0_ffn_setup():
        import jax, jax.numpy as jnp
        import numpy as np
        TOPK = 2
        HID, INTER, E, SHARED_INTER = (256, 176, 14, 352)
        key = jax.random.key(seed)
        ks = jax.random.split(key, 11)
        s = 0.02
        return {'x': jax.random.normal(ks[0], (4, 64, HID), jnp.float32), 'gate_w': jax.random.normal(ks[1], (E, HID), jnp.float32) * s, 'cls_w': jax.random.normal(ks[2], (E, HID), jnp.float32) * s, 'extra_scale': jax.random.normal(ks[3], (E,), jnp.float32) * 0.1, 'extra_bias': jax.random.normal(ks[4], (E,), jnp.float32) * 0.01, 'wg': jax.random.normal(ks[5], (E, INTER, HID), jnp.float32) * s, 'wu': jax.random.normal(ks[6], (E, INTER, HID), jnp.float32) * s, 'wd': jax.random.normal(ks[7], (E, HID, INTER), jnp.float32) * s, 'sg': jax.random.normal(ks[8], (SHARED_INTER, HID), jnp.float32) * s, 'su': jax.random.normal(ks[9], (SHARED_INTER, HID), jnp.float32) * s, 'sd': jax.random.normal(ks[10], (HID, SHARED_INTER), jnp.float32) * s}
    _L0_ffn_all = _L0_ffn_setup()
    _L0_ffn_in = {k: v for k, v in _L0_ffn_all.items() if k in ('gate_w', 'cls_w', 'extra_scale', 'extra_bias', 'wg', 'wu', 'wd', 'sg', 'su', 'sd')}
    del _L0_ffn_all

    def _L1_xattn_setup():
        import jax, jax.numpy as jnp
        import numpy as np
        key = jax.random.key(seed)
        ks = jax.random.split(key, 6)
        B, L, N, C, D = (8, 64, 256, 128, 128)
        return {'teacher_logits': jax.random.normal(ks[0], (B, L, N), dtype=jnp.float32), 'teacher_features': jax.random.normal(ks[1], (B, N, C), dtype=jnp.float32), 'Wq': jax.random.normal(ks[2], (D, C), dtype=jnp.float32) * (1.0 / np.sqrt(C)), 'bq': jnp.zeros((D,), dtype=jnp.float32), 'Wk': jax.random.normal(ks[3], (D, C), dtype=jnp.float32) * (1.0 / np.sqrt(C)), 'bk': jnp.zeros((D,), dtype=jnp.float32)}
    _L1_xattn_all = _L1_xattn_setup()
    _L1_xattn_in = {k: v for k, v in _L1_xattn_all.items() if k in ('Wq', 'bq', 'Wk', 'bk')}
    del _L1_xattn_all

    def _L1_ffn_setup():
        import jax, jax.numpy as jnp
        import numpy as np
        EPS = 1e-05

        def _act_quant(x, bits=8):
            qb = float(2 ** (bits - 1) - 1)
            scale = qb / jnp.clip(jnp.max(jnp.abs(x), axis=-1, keepdims=True), EPS, None)
            x_dq = jnp.clip(jnp.round(x * scale), -qb, qb) / scale
            return x + jax.lax.stop_gradient(x_dq - x)

        def _weight_quant(w):
            s = jnp.clip(jnp.mean(jnp.abs(w)), EPS, None)
            w_dq = jnp.clip(jnp.round(w / s), -1.0, 1.0) * s
            return w + jax.lax.stop_gradient(w_dq - w)

        def _bitlinear(x, w, bits=8):
            return jnp.einsum('bsi,oi->bso', _act_quant(x, bits), _weight_quant(w))
        key = jax.random.key(seed)
        k1, k2, k3 = jax.random.split(key, 3)
        B, S, H = (4, 512, 256)
        I = int(H * 2.0)
        return {'hidden_states': jax.random.normal(k1, (B, S, H), dtype=jnp.float32), 'w_up': jax.random.normal(k2, (I, H), dtype=jnp.float32) * (1.0 / np.sqrt(H)), 'w_down': jax.random.normal(k3, (H, I), dtype=jnp.float32) * (1.0 / np.sqrt(I))}
    _L1_ffn_all = _L1_ffn_setup()
    _L1_ffn_in = {k: v for k, v in _L1_ffn_all.items() if k in ('w_up', 'w_down')}
    del _L1_ffn_all

    def _L2_xattn_setup():
        import jax, jax.numpy as jnp
        import numpy as np
        B, S1, S2, DCA = (2, 256, 128, 16)
        QDIM, KDIM, H = (256, 128, 16)
        HD = QDIM // H
        SCALE = HD ** (-0.5)
        EPS = 1e-06
        DCA_WEIGHT = 1.0

        def _ln(t, w, b):
            m = jnp.mean(t, axis=-1, keepdims=True)
            v = jnp.var(t, axis=-1, keepdims=True)
            return (t - m) * jax.lax.rsqrt(v + EPS) * w + b

        def _attn(q, k, v):
            s = jnp.einsum('bhqd,bhkd->bhqk', q, k) * SCALE
            p = jax.nn.softmax(s, axis=-1)
            return jnp.einsum('bhqk,bhkd->bhqd', p, v)
        key = jax.random.key(seed)
        ks = jax.random.split(key, 8)
        w = lambda k, shape: jax.random.normal(k, shape, jnp.float32) * 0.02
        return {'x': jax.random.normal(ks[0], (B, S1, QDIM), jnp.float32), 'y': jax.random.normal(ks[1], (B, S2 + DCA, KDIM), jnp.float32), 'Wq': w(ks[2], (QDIM, QDIM)), 'bq': jnp.zeros((QDIM,), jnp.float32), 'Wk': w(ks[3], (KDIM, QDIM)), 'bk': jnp.zeros((QDIM,), jnp.float32), 'Wv': w(ks[4], (KDIM, QDIM)), 'bv': jnp.zeros((QDIM,), jnp.float32), 'Wkv_dca': w(ks[5], (KDIM, 2 * QDIM)), 'bkv_dca': jnp.zeros((2 * QDIM,), jnp.float32), 'qn_w': jnp.ones((HD,), jnp.float32), 'qn_b': jnp.zeros((HD,), jnp.float32), 'kn_w': jnp.ones((HD,), jnp.float32), 'kn_b': jnp.zeros((HD,), jnp.float32), 'kn_dca_w': jnp.ones((HD,), jnp.float32), 'kn_dca_b': jnp.zeros((HD,), jnp.float32), 'Wo': w(ks[6], (QDIM, QDIM)), 'bo': jnp.zeros((QDIM,), jnp.float32)}
    _L2_xattn_all = _L2_xattn_setup()
    _L2_xattn_in = {k: v for k, v in _L2_xattn_all.items() if k in ('Wq', 'bq', 'Wk', 'bk', 'Wv', 'bv', 'Wkv_dca', 'bkv_dca', 'qn_w', 'qn_b', 'kn_w', 'kn_b', 'kn_dca_w', 'kn_dca_b', 'Wo', 'bo')}
    del _L2_xattn_all

    def _L2_ffn_setup():
        import jax, jax.numpy as jnp
        import numpy as np
        _FP8_DTYPE = jnp.float8_e4m3fn
        _FP8_MAX = 448.0
        key = jax.random.key(seed)
        k_x, k_w = jax.random.split(key)
        B, S, IN, OUT = (2, 1024, 256, 256)
        x = jax.random.normal(k_x, (B, S, IN), dtype=jnp.float32)
        w_f32 = jax.random.normal(k_w, (OUT, IN), dtype=jnp.float32) * 0.02
        weight = w_f32.astype(_FP8_DTYPE)
        weight_scale = jnp.asarray(1.5, dtype=jnp.float32)
        input_scale = jnp.asarray(0.75, dtype=jnp.bfloat16)
        return {'x': x, 'weight': weight, 'weight_scale': weight_scale, 'input_scale': input_scale}
    _L2_ffn_all = _L2_ffn_setup()
    _L2_ffn_in = {k: v for k, v in _L2_ffn_all.items() if k in ('weight', 'weight_scale', 'input_scale')}
    del _L2_ffn_all

    def _L3_xattn_setup():
        import jax, jax.numpy as jnp
        import numpy as np
        EPS = 1e-05

        def rmsnorm(x, g, eps=EPS):
            var = jnp.mean(jnp.square(x), axis=-1, keepdims=True)
            return x * jax.lax.rsqrt(var + eps) * g
        key = jax.random.key(seed)
        ks = jax.random.split(key, 8)
        B, Sq, Skv = (2, 512, 64)
        dim, cdim, H, D = (256, 128, 16, 128)
        inner = H * D
        s = lambda f: 1.0 / np.sqrt(f)
        return {'hidden_states': jax.random.normal(ks[0], (B, Sq, dim), jnp.float32), 'encoder_hidden_states': jax.random.normal(ks[1], (B, Skv, cdim), jnp.float32), 'Wq': jax.random.normal(ks[2], (dim, inner), jnp.float32) * s(dim), 'Wk': jax.random.normal(ks[3], (cdim, inner), jnp.float32) * s(cdim), 'Wv': jax.random.normal(ks[4], (cdim, inner), jnp.float32) * s(cdim), 'Wo': jax.random.normal(ks[5], (inner, dim), jnp.float32) * s(inner), 'gq': jnp.ones((D,), jnp.float32), 'gk': jnp.ones((D,), jnp.float32)}
    _L3_xattn_all = _L3_xattn_setup()
    _L3_xattn_in = {k: v for k, v in _L3_xattn_all.items() if k in ('Wq', 'Wk', 'Wv', 'Wo', 'gq', 'gk')}
    del _L3_xattn_all

    def _L3_ffn_setup():
        import jax, jax.numpy as jnp
        import numpy as np
        import math
        GOLDEN_CENTER = 1.0 / math.e
        GOLDEN_LOWER = 0.5 - math.log(4.0 / 3.0)
        GOLDEN_UPPER = 0.5
        B, T, D = (4, 128, 256)
        E = 8
        F = 1024 // (E // 2)
        R = 64
        NL = 2

        def _router_weights(x, Wr, temperature):
            logits = jnp.einsum('btd,de->bte', x, Wr)
            inhibition = jax.nn.sigmoid(logits / temperature)
            in_zone = (inhibition >= GOLDEN_LOWER) & (inhibition <= GOLDEN_UPPER)
            distance = jnp.abs(inhibition - GOLDEN_CENTER)
            w = jnp.exp(-distance / 0.1) * in_zone.astype(x.dtype)
            wsum = w.sum(axis=-1, keepdims=True)
            no_expert = wsum < 1e-08
            fb = jnp.exp(-distance / 0.3)
            _, top2 = jax.lax.top_k(fb, 2)
            fb_mask = jax.nn.one_hot(top2, E, dtype=x.dtype).sum(axis=-2)
            fb_w = fb * fb_mask
            fb_w = fb_w / jnp.clip(fb_w.sum(axis=-1, keepdims=True), 1e-08)
            w = jnp.where(no_expert, fb_w, w)
            return w / jnp.clip(w.sum(axis=-1, keepdims=True), 1e-08)
        key = jax.random.key(seed)
        ks = jax.random.split(key, 13)
        s = 0.02
        x = jax.random.normal(ks[0], (B, T, D), dtype=jnp.float32)
        Wg = jax.random.normal(ks[1], (E, D, F), dtype=jnp.float32) * s
        Wu = jax.random.normal(ks[2], (E, D, F), dtype=jnp.float32) * s
        Wd = jax.random.normal(ks[3], (E, F, D), dtype=jnp.float32) * s
        Ga = jax.random.normal(ks[4], (NL, D, R), dtype=jnp.float32) * s
        Gb = jax.random.normal(ks[5], (NL, R, F), dtype=jnp.float32) * s
        Ua = jax.random.normal(ks[6], (NL, D, R), dtype=jnp.float32) * s
        Ub = jax.random.normal(ks[7], (NL, R, F), dtype=jnp.float32) * s
        Da = jax.random.normal(ks[8], (NL, F, R), dtype=jnp.float32) * s
        Db = jax.random.normal(ks[9], (NL, R, D), dtype=jnp.float32) * s
        Wr = jax.random.normal(ks[10], (D, E), dtype=jnp.float32) * s
        temperature = jnp.ones((1,), dtype=jnp.float32)
        return {'x': x, 'Wg': Wg, 'Wu': Wu, 'Wd': Wd, 'Ga': Ga, 'Gb': Gb, 'Ua': Ua, 'Ub': Ub, 'Da': Da, 'Db': Db, 'Wr': Wr, 'temperature': temperature}
    _L3_ffn_all = _L3_ffn_setup()
    _L3_ffn_in = {k: v for k, v in _L3_ffn_all.items() if k in ('Wg', 'Wu', 'Wd', 'Ga', 'Gb', 'Ua', 'Ub', 'Da', 'Db', 'Wr', 'temperature')}
    del _L3_ffn_all
    return {'x': x, 'fside_BxS2xS2_0': fside_BxS2xS2_0, 'ctx_1024': ctx_1024, 'L0_ffn_gate_w': _L0_ffn_in['gate_w'], 'L0_ffn_cls_w': _L0_ffn_in['cls_w'], 'L0_ffn_extra_scale': _L0_ffn_in['extra_scale'], 'L0_ffn_extra_bias': _L0_ffn_in['extra_bias'], 'L0_ffn_wg': _L0_ffn_in['wg'], 'L0_ffn_wu': _L0_ffn_in['wu'], 'L0_ffn_wd': _L0_ffn_in['wd'], 'L0_ffn_sg': _L0_ffn_in['sg'], 'L0_ffn_su': _L0_ffn_in['su'], 'L0_ffn_sd': _L0_ffn_in['sd'], 'L1_xattn_Wq': _L1_xattn_in['Wq'], 'L1_xattn_bq': _L1_xattn_in['bq'], 'L1_xattn_Wk': _L1_xattn_in['Wk'], 'L1_xattn_bk': _L1_xattn_in['bk'], 'L1_ffn_w_up': _L1_ffn_in['w_up'], 'L1_ffn_w_down': _L1_ffn_in['w_down'], 'L2_xattn_Wq': _L2_xattn_in['Wq'], 'L2_xattn_bq': _L2_xattn_in['bq'], 'L2_xattn_Wk': _L2_xattn_in['Wk'], 'L2_xattn_bk': _L2_xattn_in['bk'], 'L2_xattn_Wv': _L2_xattn_in['Wv'], 'L2_xattn_bv': _L2_xattn_in['bv'], 'L2_xattn_Wkv_dca': _L2_xattn_in['Wkv_dca'], 'L2_xattn_bkv_dca': _L2_xattn_in['bkv_dca'], 'L2_xattn_qn_w': _L2_xattn_in['qn_w'], 'L2_xattn_qn_b': _L2_xattn_in['qn_b'], 'L2_xattn_kn_w': _L2_xattn_in['kn_w'], 'L2_xattn_kn_b': _L2_xattn_in['kn_b'], 'L2_xattn_kn_dca_w': _L2_xattn_in['kn_dca_w'], 'L2_xattn_kn_dca_b': _L2_xattn_in['kn_dca_b'], 'L2_xattn_Wo': _L2_xattn_in['Wo'], 'L2_xattn_bo': _L2_xattn_in['bo'], 'L2_ffn_weight': _L2_ffn_in['weight'], 'L2_ffn_weight_scale': _L2_ffn_in['weight_scale'], 'L2_ffn_input_scale': _L2_ffn_in['input_scale'], 'L3_xattn_Wq': _L3_xattn_in['Wq'], 'L3_xattn_Wk': _L3_xattn_in['Wk'], 'L3_xattn_Wv': _L3_xattn_in['Wv'], 'L3_xattn_Wo': _L3_xattn_in['Wo'], 'L3_xattn_gq': _L3_xattn_in['gq'], 'L3_xattn_gk': _L3_xattn_in['gk'], 'L3_ffn_Wg': _L3_ffn_in['Wg'], 'L3_ffn_Wu': _L3_ffn_in['Wu'], 'L3_ffn_Wd': _L3_ffn_in['Wd'], 'L3_ffn_Ga': _L3_ffn_in['Ga'], 'L3_ffn_Gb': _L3_ffn_in['Gb'], 'L3_ffn_Ua': _L3_ffn_in['Ua'], 'L3_ffn_Ub': _L3_ffn_in['Ub'], 'L3_ffn_Da': _L3_ffn_in['Da'], 'L3_ffn_Db': _L3_ffn_in['Db'], 'L3_ffn_Wr': _L3_ffn_in['Wr'], 'L3_ffn_temperature': _L3_ffn_in['temperature']}

def reference(x, fside_BxS2xS2_0, ctx_1024, L0_ffn_gate_w, L0_ffn_cls_w, L0_ffn_extra_scale, L0_ffn_extra_bias, L0_ffn_wg, L0_ffn_wu, L0_ffn_wd, L0_ffn_sg, L0_ffn_su, L0_ffn_sd, L1_xattn_Wq, L1_xattn_bq, L1_xattn_Wk, L1_xattn_bk, L1_ffn_w_up, L1_ffn_w_down, L2_xattn_Wq, L2_xattn_bq, L2_xattn_Wk, L2_xattn_bk, L2_xattn_Wv, L2_xattn_bv, L2_xattn_Wkv_dca, L2_xattn_bkv_dca, L2_xattn_qn_w, L2_xattn_qn_b, L2_xattn_kn_w, L2_xattn_kn_b, L2_xattn_kn_dca_w, L2_xattn_kn_dca_b, L2_xattn_Wo, L2_xattn_bo, L2_ffn_weight, L2_ffn_weight_scale, L2_ffn_input_scale, L3_xattn_Wq, L3_xattn_Wk, L3_xattn_Wv, L3_xattn_Wo, L3_xattn_gq, L3_xattn_gk, L3_ffn_Wg, L3_ffn_Wu, L3_ffn_Wd, L3_ffn_Ga, L3_ffn_Gb, L3_ffn_Ua, L3_ffn_Ub, L3_ffn_Da, L3_ffn_Db, L3_ffn_Wr, L3_ffn_temperature):
    import jax
    import jax.numpy as jnp

    def _L0_xattn_ref(x, gate_up_weight, down_weight):
        import jax, jax.numpy as jnp
        import numpy as np
        EPS = 1e-06
        QMAX = 127.0

        def _smooth_quant_linear(x, w):
            amax_x = jnp.max(jnp.abs(x), axis=0)
            amax_w = jnp.max(jnp.abs(w), axis=0)
            s = jnp.sqrt(jnp.maximum(amax_x, EPS) / jnp.maximum(amax_w, EPS))
            s = jnp.maximum(s, EPS)
            xs = x / s
            ws = w * s
            x_scale = jnp.maximum(jnp.max(jnp.abs(xs), axis=-1, keepdims=True), EPS) / QMAX
            w_scale = jnp.maximum(jnp.max(jnp.abs(ws), axis=-1, keepdims=True), EPS) / QMAX
            x_q = jnp.clip(jnp.round(xs / x_scale), -QMAX, QMAX)
            w_q = jnp.clip(jnp.round(ws / w_scale), -QMAX, QMAX)
            return x_q @ w_q.T * x_scale * w_scale.T

        def _expert_forward(xe, guw, dw):
            h = _smooth_quant_linear(xe, guw)
            gate, up = jnp.split(h, 2, axis=-1)
            a = jax.nn.silu(gate) * up
            return _smooth_quant_linear(a, dw)
        return jax.vmap(_expert_forward)(x, gate_up_weight, down_weight)

    def _L0_ffn_ref(x, gate_w, cls_w, extra_scale, extra_bias, wg, wu, wd, sg, su, sd):
        import jax, jax.numpy as jnp
        import numpy as np
        TOPK = 2
        HID, INTER, E, SHARED_INTER = (256, 176, 14, 352)
        shape = x.shape
        d = shape[-1]
        xf = x.reshape(-1, d)
        T = xf.shape[0]
        n_exp = gate_w.shape[0]
        logits = xf @ cls_w.T * jax.nn.silu(xf @ gate_w.T)
        scores = jax.nn.softmax(jnp.abs(logits).astype(jnp.float32), axis=-1)
        biased = scores + extra_bias[None, :]
        _, idx = jax.lax.top_k(biased, TOPK)
        orig = 1.0 + scores * extra_scale[None, :]
        w = jnp.take_along_axis(orig, idx, axis=1).astype(x.dtype)
        combine = jnp.zeros((T, n_exp), x.dtype).at[jnp.arange(T)[:, None], idx].add(w)
        g = jax.nn.silu(jnp.einsum('td,efd->etf', xf, wg))
        u = jnp.einsum('td,efd->etf', xf, wu)
        o = jnp.einsum('etf,edf->etd', g * u, wd)
        y = jnp.einsum('etd,te->td', o, combine)
        z = jax.nn.silu(xf @ sg.T) * (xf @ su.T) @ sd.T
        return (y + z).reshape(shape)

    def _L1_xattn_ref(teacher_logits, teacher_features, Wq, bq, Wk, bk):
        import jax, jax.numpy as jnp
        import numpy as np
        query = jnp.einsum('bnc,dc->bnd', teacher_features, Wq) + bq
        key = jnp.einsum('bnc,dc->bnd', teacher_features, Wk) + bk
        energy = jnp.einsum('bnd,bmd->bnm', query, key)
        attention = jax.nn.softmax(energy, axis=-1)
        x_m = jnp.einsum('bln,bmn->blm', teacher_logits, attention)
        return x_m

    def _L1_ffn_ref(hidden_states, w_up, w_down):
        import jax, jax.numpy as jnp
        import numpy as np
        EPS = 1e-05

        def _act_quant(x, bits=8):
            qb = float(2 ** (bits - 1) - 1)
            scale = qb / jnp.clip(jnp.max(jnp.abs(x), axis=-1, keepdims=True), EPS, None)
            x_dq = jnp.clip(jnp.round(x * scale), -qb, qb) / scale
            return x + jax.lax.stop_gradient(x_dq - x)

        def _weight_quant(w):
            s = jnp.clip(jnp.mean(jnp.abs(w)), EPS, None)
            w_dq = jnp.clip(jnp.round(w / s), -1.0, 1.0) * s
            return w + jax.lax.stop_gradient(w_dq - w)

        def _bitlinear(x, w, bits=8):
            return jnp.einsum('bsi,oi->bso', _act_quant(x, bits), _weight_quant(w))
        bits = 8
        h = _bitlinear(hidden_states, w_up, bits)
        h = jnp.square(jax.nn.relu(h))
        out = _bitlinear(h, w_down, bits)
        return out

    def _L2_xattn_ref(x, y, Wq, bq, Wk, bk, Wv, bv, Wkv_dca, bkv_dca, qn_w, qn_b, kn_w, kn_b, kn_dca_w, kn_dca_b, Wo, bo):
        import jax, jax.numpy as jnp
        import numpy as np
        B, S1, S2, DCA = (2, 256, 128, 16)
        QDIM, KDIM, H = (256, 128, 16)
        HD = QDIM // H
        SCALE = HD ** (-0.5)
        EPS = 1e-06
        DCA_WEIGHT = 1.0

        def _ln(t, w, b):
            m = jnp.mean(t, axis=-1, keepdims=True)
            v = jnp.var(t, axis=-1, keepdims=True)
            return (t - m) * jax.lax.rsqrt(v + EPS) * w + b

        def _attn(q, k, v):
            s = jnp.einsum('bhqd,bhkd->bhqk', q, k) * SCALE
            p = jax.nn.softmax(s, axis=-1)
            return jnp.einsum('bhqk,bhkd->bhqd', p, v)
        b, s1, _ = x.shape
        y_dca = y[:, -DCA:, :]
        y_main = y[:, :-DCA, :]
        kv_dca = (y_dca @ Wkv_dca + bkv_dca).reshape(b, DCA, 2, H, HD)
        k_dca = _ln(kv_dca[:, :, 0], kn_dca_w, kn_dca_b)
        v_dca = kv_dca[:, :, 1]
        s2 = y_main.shape[1]
        q = _ln((x @ Wq + bq).reshape(b, s1, H, HD), qn_w, qn_b)
        kv = jnp.concatenate([y_main @ Wk + bk, y_main @ Wv + bv], axis=-1)
        kv = kv.reshape(b, s2, H, 2 * HD)
        k = _ln(kv[..., :HD], kn_w, kn_b)
        v = kv[..., HD:]
        qT = q.transpose(0, 2, 1, 3)
        ctx = _attn(qT, k.transpose(0, 2, 1, 3), v.transpose(0, 2, 1, 3))
        ctx = ctx.transpose(0, 2, 1, 3).reshape(b, s1, QDIM)
        ctx_dca = _attn(qT, k_dca.transpose(0, 2, 1, 3), v_dca.transpose(0, 2, 1, 3))
        ctx_dca = ctx_dca.transpose(0, 2, 1, 3).reshape(b, s1, QDIM)
        ctx = ctx + DCA_WEIGHT * ctx_dca
        return ctx @ Wo + bo

    def _L2_ffn_ref(x, weight, weight_scale, input_scale):
        import jax, jax.numpy as jnp
        import numpy as np
        _FP8_DTYPE = jnp.float8_e4m3fn
        _FP8_MAX = 448.0
        orig_dtype = x.dtype
        w = weight.astype(orig_dtype) * weight_scale.astype(orig_dtype)
        s_f32 = input_scale.astype(jnp.float32)
        x_scaled = x.astype(jnp.float32) / s_f32
        x_fp8 = jnp.clip(x_scaled, -_FP8_MAX, _FP8_MAX).astype(_FP8_DTYPE)
        x_qdq = x_fp8.astype(orig_dtype) * s_f32.astype(orig_dtype)
        return jnp.einsum('bsi,oi->bso', x_qdq, w)

    def _L3_xattn_ref(hidden_states, encoder_hidden_states, Wq, Wk, Wv, Wo, gq, gk):
        import jax, jax.numpy as jnp
        import numpy as np
        EPS = 1e-05

        def rmsnorm(x, g, eps=EPS):
            var = jnp.mean(jnp.square(x), axis=-1, keepdims=True)
            return x * jax.lax.rsqrt(var + eps) * g
        B, Sq, _ = hidden_states.shape
        Skv = encoder_hidden_states.shape[1]
        D = gq.shape[0]
        H = Wq.shape[1] // D
        scale = 1.0 / np.sqrt(D)
        q = (hidden_states @ Wq).reshape(B, Sq, H, D)
        k = (encoder_hidden_states @ Wk).reshape(B, Skv, H, D)
        v = (encoder_hidden_states @ Wv).reshape(B, Skv, H, D)
        q = rmsnorm(q, gq)
        k = rmsnorm(k, gk)
        scores = jnp.einsum('bqhd,bkhd->bhqk', q, k) * scale
        attn = jax.nn.softmax(scores, axis=-1)
        out = jnp.einsum('bhqk,bkhd->bqhd', attn, v)
        out = out.reshape(B, Sq, H * D)
        return out @ Wo

    def _L3_ffn_ref(x, Wg, Wu, Wd, Ga, Gb, Ua, Ub, Da, Db, Wr, temperature):
        import jax, jax.numpy as jnp
        import numpy as np
        import math
        GOLDEN_CENTER = 1.0 / math.e
        GOLDEN_LOWER = 0.5 - math.log(4.0 / 3.0)
        GOLDEN_UPPER = 0.5
        B, T, D = (4, 128, 256)
        E = 8
        F = 1024 // (E // 2)
        R = 64
        NL = 2

        def _router_weights(x, Wr, temperature):
            logits = jnp.einsum('btd,de->bte', x, Wr)
            inhibition = jax.nn.sigmoid(logits / temperature)
            in_zone = (inhibition >= GOLDEN_LOWER) & (inhibition <= GOLDEN_UPPER)
            distance = jnp.abs(inhibition - GOLDEN_CENTER)
            w = jnp.exp(-distance / 0.1) * in_zone.astype(x.dtype)
            wsum = w.sum(axis=-1, keepdims=True)
            no_expert = wsum < 1e-08
            fb = jnp.exp(-distance / 0.3)
            _, top2 = jax.lax.top_k(fb, 2)
            fb_mask = jax.nn.one_hot(top2, E, dtype=x.dtype).sum(axis=-2)
            fb_w = fb * fb_mask
            fb_w = fb_w / jnp.clip(fb_w.sum(axis=-1, keepdims=True), 1e-08)
            w = jnp.where(no_expert, fb_w, w)
            return w / jnp.clip(w.sum(axis=-1, keepdims=True), 1e-08)
        weights = _router_weights(x, Wr, temperature)
        gate = jnp.einsum('btd,edf->ebtf', x, Wg)
        up = jnp.einsum('btd,edf->ebtf', x, Wu)
        gate = gate.at[:NL].add(jnp.einsum('btd,edr,erf->ebtf', x, Ga, Gb))
        up = up.at[:NL].add(jnp.einsum('btd,edr,erf->ebtf', x, Ua, Ub))
        mid = jax.nn.silu(gate) * up
        out = jnp.einsum('ebtf,efd->ebtd', mid, Wd)
        out = out.at[:NL].add(jnp.einsum('ebtf,efr,erd->ebtd', mid[:NL], Da, Db))
        return jnp.einsum('bte,ebtd->btd', weights, out)
    x = x + _L0_xattn_ref(_layernorm(x, axis=-1), fside_BxS2xS2_0, ctx_1024)
    x = x + _L0_ffn_ref(_layernorm(x, axis=-1), L0_ffn_gate_w, L0_ffn_cls_w, L0_ffn_extra_scale, L0_ffn_extra_bias, L0_ffn_wg, L0_ffn_wu, L0_ffn_wd, L0_ffn_sg, L0_ffn_su, L0_ffn_sd)
    x = x + _L1_xattn_ref(_layernorm(x, axis=-1), ctx_1024, L1_xattn_Wq, L1_xattn_bq, L1_xattn_Wk, L1_xattn_bk)
    x = x + _L1_ffn_ref(_layernorm(x, axis=-1), L1_ffn_w_up, L1_ffn_w_down)
    x = x + _L2_xattn_ref(_layernorm(x, axis=-1), ctx_1024, L2_xattn_Wq, L2_xattn_bq, L2_xattn_Wk, L2_xattn_bk, L2_xattn_Wv, L2_xattn_bv, L2_xattn_Wkv_dca, L2_xattn_bkv_dca, L2_xattn_qn_w, L2_xattn_qn_b, L2_xattn_kn_w, L2_xattn_kn_b, L2_xattn_kn_dca_w, L2_xattn_kn_dca_b, L2_xattn_Wo, L2_xattn_bo)
    x = x + _L2_ffn_ref(_layernorm(x, axis=-1), L2_ffn_weight, L2_ffn_weight_scale, L2_ffn_input_scale)
    x = x + _L3_xattn_ref(_layernorm(x, axis=-1), ctx_1024, L3_xattn_Wq, L3_xattn_Wk, L3_xattn_Wv, L3_xattn_Wo, L3_xattn_gq, L3_xattn_gk)
    x = x + _L3_ffn_ref(_layernorm(x, axis=-1), L3_ffn_Wg, L3_ffn_Wu, L3_ffn_Wd, L3_ffn_Ga, L3_ffn_Gb, L3_ffn_Ua, L3_ffn_Ub, L3_ffn_Da, L3_ffn_Db, L3_ffn_Wr, L3_ffn_temperature)
    return x

_drawn_inputs = setup_inputs


def setup_inputs(seed=0):
    import zlib

    import numpy as np

    out = dict(_drawn_inputs(seed))
    spreads = {'L1_xattn_bq': (0.0, 0.8),
     'L1_xattn_bk': (0.0, 2.0),
     'L2_xattn_bq': (0.0, 2.0),
     'L2_xattn_bk': (0.0, 0.675),
     'L2_xattn_bv': (0.0, 0.638),
     'L2_xattn_bkv_dca': (0.0, 0.467),
     'L2_xattn_qn_w': (1.0, 0.6),
     'L2_xattn_qn_b': (0.0, 0.8),
     'L2_xattn_kn_w': (1.0, 0.6),
     'L2_xattn_kn_b': (0.0, 2.0),
     'L2_xattn_kn_dca_w': (1.0, 0.6),
     'L2_xattn_kn_dca_b': (0.0, 2.0),
     'L2_xattn_bo': (0.0, 0.1),
     'L3_xattn_gq': (1.0, 0.6),
     'L3_xattn_gk': (1.0, 0.6)}
    factors = {'fside_BxS2xS2_0': 4.921,
     'ctx_1024': 4.502,
     'L0_ffn_gate_w': 5.815,
     'L0_ffn_cls_w': 5.767,
     'L0_ffn_extra_scale': 8.0,
     'L0_ffn_extra_bias': 3.815,
     'L0_ffn_wg': 3.56,
     'L0_ffn_wu': 3.529,
     'L0_ffn_wd': 3.506,
     'L0_ffn_sg': 3.545,
     'L0_ffn_su': 3.508,
     'L0_ffn_sd': 3.532,
     'L1_xattn_Wq': 8.0,
     'L1_xattn_Wk': 8.0,
     'L2_xattn_Wq': 8.0,
     'L2_xattn_Wk': 8.0,
     'L2_xattn_Wv': 8.0,
     'L2_xattn_Wkv_dca': 8.0,
     'L3_xattn_Wq': 8.0,
     'L3_xattn_Wk': 8.0,
     'L3_xattn_Wv': 8.0,
     'L3_xattn_Wo': 8.0,
     'L3_ffn_Wg': 8.0,
     'L3_ffn_Wu': 8.0,
     'L3_ffn_Wd': 8.0,
     'L3_ffn_Ga': 8.0,
     'L3_ffn_Gb': 8.0,
     'L3_ffn_Ua': 8.0,
     'L3_ffn_Ub': 8.0,
     'L3_ffn_Da': 8.0,
     'L3_ffn_Db': 8.0,
     'L3_ffn_Wr': 8.0}
    for name, (base, spread) in spreads.items():
        noise = np.random.default_rng([zlib.crc32(name.encode()), seed]).standard_normal(out[name].shape)
        drawn = base * np.exp(spread * noise) if base else spread * noise
        out[name] = jnp.asarray(drawn.astype(out[name].dtype))
    for name, factor in factors.items():
        out[name] = (out[name] * factor).astype(out[name].dtype)
    return out
```

```python
import concourse.bass as bass
from concourse import mybir
from contextlib import ExitStack

B, S, D, C = 4, 256, 256, 128
NT = B * S // 128
KD = D // 128
E0, I0, SH0 = 14, 176, 352
F0 = E0 * I0 + SH0
NJ0 = F0 // 128
E3, I3 = 8, 256
F3 = E3 * I3
NJ3 = F3 // 128
NLORA, RANK = 2, 64
CH = 3 * D
K0, K3 = 3 * (E0 + 1), 3 * E3
H2, HD2, DCA = 16, 16, 16
VE = 2 * (HD2 + 1)
H3, HD3 = 16, 128
HG = 4
NG = B * H3 // HG
MAGIC = 1.5 * 2.0 ** 23
RING = 4
LN_EPS = 1e-5


def program(nc, x, ident, sel0, sel3, selr, masks, iota, gu_t, ctx_t, ctx, w_rt, rt_aff, w_ffn0,
            l1_w, l1_b, w_up, w_dn, l2_q, l2_kv, l2_dca, l2_o, l2_aff, w8, w8_sc, in_sc,
            l3_q, l3_k, l3_v, l3_o, l3_g, w_ffn3, lo_a, lo_b, lo_da, lo_db, w_r3, temp, out):
    dt = mybir.dt
    f32, f16, bf16, i32, u32, u8 = dt.float32, dt.float16, dt.bfloat16, dt.int32, dt.uint32, dt.uint8
    ALU, ACT, AX = mybir.AluOpType, mybir.ActivationFunctionType, mybir.AxisListType

    ctxs = ExitStack()
    with ctxs:
        def sb(name, shape, d):
            return ctxs.enter_context(nc.sbuf_tensor(name, shape, d))

        def sem(name):
            return ctxs.enter_context(nc.semaphore(name))

        def cut(region, at, shape, d):
            n = 1
            for s in shape:
                n *= s
            size = {f32: 4, i32: 4, u32: 4, f16: 2, bf16: 2, u8: 1}[d]
            v = region[:, at // 4:(at + n * size + 3) // 4]
            if d != f32:
                v = v.bitcast(d)
            if len(shape) == 2:
                v = v.rearrange("p (a b) -> p a b", a=shape[0])
            elif len(shape) == 3:
                v = v.rearrange("p (a b c) -> p a b c", a=shape[0], b=shape[1])
            elif len(shape) == 4:
                v = v.rearrange("p (a b c d) -> p a b c d", a=shape[0], b=shape[1], c=shape[2])
            return v, at + n * size

        X = sb("X", [128, NT, D], f32)
        XNr = sb("XN", [128, NT * D], f32)
        XN = XNr[:, :].rearrange("p (t d) -> p t d", t=NT)
        XTh = sb("XTh", [128, KD, B * S], f16)
        XTl = sb("XTl", [128, KD, B * S], f16)
        R1 = sb("R1", [128, NJ0 * CH], f32)
        R2 = sb("R2", [128, NJ3 * CH], f32)
        R3 = sb("R3", [128, 3584], f32)
        R4 = sb("R4", [128, 3072], f32)
        ring = sb("ring", [128, RING, CH], f32)
        idf = sb("idf", [128, 128], f32)
        idb = sb("idb", [128, 128], bf16)
        idh = sb("idh", [128, 128], f16)
        onesf = sb("onesf", [128, 128], f32)
        magic = sb("magic", [128, 1], f32)
        sel0b = sb("sel0b", [K0, F0], bf16)
        sel3b = sb("sel3b", [K3, F3], bf16)
        combT = sb("combT", [K0, B * S], bf16)
        CTh = sb("CTh", [128, B, S], f16)
        CTl = sb("CTl", [128, B, S], f16)
        small = sb("small", [128, 64], f32)
        st = sb("st", [128, NT, 6], f32)
        mv = sb("mv", [128, NT, 2], f32)
        nw = sb("nw", [128, 5, 128], f32)

        PS = [ctxs.enter_context(nc.psum_tensor(f"PS{i}", [128, 512], f32)) for i in range(8)]

        guT, o = cut(R2, 0, [B, KD, S], f32)
        ctT, o = cut(R2, o, [B, S], f32)
        QS, o = cut(R2, o, [B, 4, S], f32)
        QB, o = cut(R2, o, [B, 4, S], bf16)
        QTt, o = cut(R2, o, [B, 4, S], bf16)
        assert o <= NJ3 * CH * 4, o
        HU, o = cut(R3, 0, [B, 2, S], f32)
        HA, o = cut(R3, o, [B, 2, 128], f32)
        DG, o = cut(R4, 0, [B, 2, 128], f32)
        WB, o = cut(R4, o, [B, S], f32)
        sq = sb("sq", [128, B, 32], f32)

        W0h, o = cut(R1, 0, [NJ0, CH], f16)
        W0l, o = cut(R1, o, [NJ0, CH], f16)
        W3h, o = cut(R2, 0, [NJ3, CH], f16)
        W3l, o = cut(R2, o, [NJ3, CH], f16)
        SI, o = cut(R3, 0, [2, 512], f32)
        T1, o = cut(R3, o, [2, 512], f32)
        T2, o = cut(R3, o, [512], f32)
        Hh, o = cut(R3, o, [2, 512], f16)
        Hl, o = cut(R3, o, [2, 512], f16)
        QK1h, o = cut(R2, 0, [B, 2, S], f16)
        QK1l, o = cut(R2, o, [B, 2, S], f16)
        EX1, o = cut(R2, o, [B, 2, S], f32)
        AT1h, o = cut(R2, o, [B, 2, S], f16)
        AT1l, o = cut(R2, o, [B, 2, S], f16)
        TWu, o = cut(R2, o, [KD, 512], bf16)
        TWd, o = cut(R2, o, [4, D], bf16)
        rawU, o = cut(R2, o, [KD * 512], f32)
        rawD, o = cut(R2, o, [4 * D], f32)
        assert o <= NJ3 * CH * 4, o
        HR1, o = cut(R1, 0, [B, 2, 512], f32)
        HQ1, o = cut(R1, o, [B, 2, 512], bf16)
        HT1, o = cut(R1, o, [B, 4, S], bf16)
        XF1, o = cut(R1, o, [B, 2, D], f32)
        XQ1, o = cut(R1, o, [B, 2, D], bf16)
        XQT1, o = cut(R1, o, [B, KD, S], bf16)
        KT3, o = cut(R1, 0, [B, H2 // 2, S], f16)
        QT3, o = cut(R1, o, [B, H2 // 2, S], f16)
        VEh, o = cut(R1, o, [2, B, H2, VE], f16)
        VEl, o = cut(R1, o, [2, B, H2, VE], f16)
        HS2, o = cut(R1, o, [B, 2, H2, 64], f16)
        assert o <= NJ0 * CH * 4, o
        BKV, o = cut(R2, 8192, [2, 2 * D], f32)
        BQO, o = cut(R2, o, [2, D], f32)
        OB2, o = cut(R2, o, [2, H2, VE], f32)
        CX2, o = cut(R2, o, [2, D], f32)
        CXh, o = cut(R2, o, [KD, S], f16)
        CXl, o = cut(R2, o, [KD, S], f16)
        KG2, o = cut(R2, o, [2, 2, HD2], f32)
        QG2, o = cut(R2, o, [2, HD2], f32)
        Eh2, o = cut(R2, o, [4, 512], f16)
        KF, o = cut(R2, o, [B, 2, D], f32)
        VF, o = cut(R2, o, [2, B, D], f32)
        TM2, o = cut(R2, o, [2 * D], f32)
        assert o <= NJ3 * CH * 4, o
        TM4, o = cut(R3, 0, [B * 2, H2, HD2], f32)
        EX2, o = cut(R3, 0, [4, 512], f32)
        El2, o = cut(R3, o, [4, 512], f16)
        W2h, o = cut(R4, 0, [4, 2 * D], f16)
        W2l, o = cut(R4, o, [4, 2 * D], f16)
        CMh, o = cut(R3, 4 * B * 2 * D, [B, 2, 128], f16)
        CMl, o = cut(R3, o, [B, 2, 128], f16)
        assert o <= 3584 * 4
        V5, o = cut(R2, 2 * 8192, [B, 2 * D], f32)
        M5, o = cut(R2, 5 * 8192, [B, 2 * D], f32)
        Q5, o = cut(R3, 0, [B, 2, D], bf16)
        QT5, o = cut(R3, o, [B, KD, S], bf16)
        W8 = sb("W8", [128, KD * D], bf16)
        w8r, o = cut(R4, 0, [KD * D], u8)
        w8i, o = cut(R4, o, [KD * D], i32)
        w8a, o = cut(R4, o, [KD * D], f32)
        w8b, o = cut(R4, o, [KD * D], f32)
        v5 = sb("v5", [128, 4], f32)
        v5b = sb("v5b", [128, 1], bf16)
        mask = sb("mask", [128, 2, 2], f32)
        W3qh, o = cut(R1, 0, [KD, H3 * HD3], f16)
        W3ql, o = cut(R1, o, [KD, H3 * HD3], f16)
        W3kh, o = cut(R1, o, [H3 * HD3], f16)
        W3kl, o = cut(R1, o, [H3 * HD3], f16)
        WVh, o = cut(R1, o, [H3, D], f16)
        WVl, o = cut(R1, o, [H3, D], f16)
        lora_at = o
        QG3h, o = cut(R1, o, [2, HG, S], f16)
        QG3l, o = cut(R1, o, [2, HG, S], f16)
        KG3h, o = cut(R1, o, [2, HG, S], f16)
        KG3l, o = cut(R1, o, [2, HG, S], f16)
        RB3, o = cut(R1, o, [2, HG, S], f32)
        assert o <= NJ0 * CH * 4, o
        LA3, o = cut(R1, lora_at, [NLORA, 2, D], f32)
        LB3, o = cut(R1, o, [NLORA, 2, I3], f32)
        LD3, o = cut(R1, o, [NLORA, I3], f32)
        LE3, o = cut(R1, o, [NLORA, D], f32)
        rawV, o = cut(R2, 8192, [H3, C], f32)
        assert o <= NJ3 * CH * 2
        rawO, o = cut(R2, NJ3 * CH * 2 + 8192, [H3, D], f32)
        assert o <= NJ3 * CH * 4
        CXTh, o = cut(R4, 8192, [B, 2, C], f16)
        CXTl, o = cut(R4, o, [B, 2, C], f16)
        SP3, o = cut(R3, 0, [2, 2, S], f32)
        PT3h, o = cut(R3, o, [2, 2, S], f16)
        PT3l, o = cut(R3, o, [2, 2, S], f16)
        OT3h, o = cut(R3, o, [2, S], f16)
        OT3l, o = cut(R3, o, [2, S], f16)
        assert o <= 3584 * 4
        SQ3, o = cut(R4, 0, [2, 2, 2 * S], f32)
        kt3 = sb("kt3", [128, 2, HG], f32)
        SR3 = sb("SR3", [3 * HG, HG * 128], bf16)
        KP3 = sb("KP3", [128, 2, 3 * HG], bf16)
        KR3 = sb("KR3", [3 * HG, S], bf16)
        g3 = sb("g3", [128, 3], f32)
        half = sb("half", [128, 1], f32)
        rs3 = sb("rs3", [128, 2, 2, 2, HG], f32)
        a3 = sb("a3", [128, 2, 8], f32)
        RV3h = sb("RV3h", [128, KD, E3], f16)
        RV3l = sb("RV3l", [128, KD, E3], f16)
        tmp3 = sb("tmp3", [128, 2], f32)
        tmpa = sb("tmpa", [128, 1], f32)
        L1Wh = sb("L1Wh", [128, 2 * C], f16)
        L1Wl = sb("L1Wl", [128, 2 * C], f16)
        b1 = sb("b1", [128, 2], f32)
        v1 = sb("v1", [128, 64], f32)
        RWh = sb("RWh", [128, KD, 2 * E0], f16)
        RWl = sb("RWl", [128, KD, 2 * E0], f16)
        iota_b = sb("iota_b", [128, 16], f32)
        rta = sb("rta", [128, 2, E0], f32)
        rt, o = cut(XNr, 0, [8, NT * 16], f32)
        idx8, o = cut(XNr, o, [NT, 8], u32)
        top8, o = cut(XNr, o, [NT, 8], f32)
        idxf, o = cut(XNr, o, [NT, 8], f32)
        CM, o = cut(XNr, o, [NT, K0], bf16)

        s_in = {n: sem(f"s_in_{n}") for n in ("x", "id", "gu", "ct", "rt", "tw", "l2", "w8", "vo", "lo", "g3")}
        s_dve, s_act, s_pool = sem("dve_order"), sem("act_order"), sem("pool_order")
        s_ln = sem("ln_done")
        s_cst = sem("constants_ready")
        s_xt = sem("sq_transposed")
        s_xs = sem("sq_x_scaled")
        s_ws = sem("sq_w_scaled")
        s_bk = sem("sq_turned_back")
        s_iv = sem("sq_steps_known")
        s_rd = sem("sq_rounded")
        s_qb = sem("sq_ints_ready")
        s_dg = sem("sq_diagonals_ready")
        s_qt = sem("sq_ints_turned")
        s_qc = sem("sq_ints_copied")
        s_pr = sem("sq_products")
        s_wb = sem("sq_w_steps_spread")
        s_hu = sem("sq_hidden")
        s_sl = sem("sq_silu")
        s_ha = sem("sq_gated")
        s_ring = [sem(f"ring_slot_{i}_loaded") for i in range(RING)]
        s_w = sem("weights_split")
        s_hi = sem("l3_weights_hi")
        s_sel = sem("selectors_ready")
        s_ft = sem("x_turned")
        s_xh = sem("x_hi_ready")
        s_xl = sem("x_lo_ready")
        s_gu = sem("ffn_gate_up")
        s_cb = sem("ffn_combine_spread")
        s_si = sem("ffn_silu")
        s_t1 = sem("ffn_gated")
        s_t2 = sem("ffn_combined")
        s_hh = sem("ffn_hidden_hi")
        s_hl = sem("ffn_hidden_lo")
        s_dn = sem("ffn_down")
        s_rp = sem("router_products")
        s_ra = sem("router_act")
        s_rv = sem("router_vector")
        s_cm = sem("combine_ready")
        s_cw = sem("combine_turned")
        s_cT = sem("combine_copied")
        s_qk = sem("l1_query_key_products")
        s_qh = sem("l1_query_key_hi")
        s_ql = sem("l1_query_key_lo")
        s_en = sem("l1_energies")
        s_mx = sem("l1_maxima")
        s_ex = sem("l1_exponentials")
        s_at = sem("l1_attention_ready")
        s_an = sem("l1_attention_normalised")
        s_tt = sem("l1_attention_turned")
        s_ah = sem("l1_attention_hi")
        s_xm = sem("l1_mixed")
        s_pa = sem("ternary_sums_partial")
        s_ps = sem("ternary_sums")
        s_tw = sem("ternary_ready")
        s_q8 = sem("l1_x_ints")
        s_qT = sem("l1_x_ints_turned")
        s_q9 = sem("l1_x_ints_copied")
        s_up = sem("l1_up")
        s_re = sem("l1_relu")
        s_v8 = sem("l1_steps_known")
        s_hs = sem("l1_hidden_scaled")
        s_h8 = sem("l1_hidden_ints")
        s_hT = sem("l1_hidden_turned")
        s_h9 = sem("l1_hidden_copied")
        s_d1 = sem("l1_down")
        s_cm2 = sem("l2_context_parts")
        s_z2 = sem("l2_pads_zeroed")
        s_kv = sem("l2_kv_products")
        s_lc = sem("l2_weights_centred")
        s_vf = sem("l2_values_biased")
        s_vh = sem("l2_values_hi")
        s_hc = sem("l2_heads_centred")
        s_hq = sem("l2_heads_squared")
        s_hn = sem("l2_heads_normalised")
        s_hp = sem("l2_heads_hi")
        s_k3 = sem("l2_heads_stacked")
        s_k4 = sem("l2_heads_turned")
        s_k5 = sem("l2_heads_copied")
        s_qp = sem("l2_query_products")
        s_s2 = sem("l2_scores")
        s_m2 = sem("l2_maxima")
        s_mt = sem("l2_maxima_turned")
        s_mc = sem("l2_maxima_copied")
        s_st = sem("l2_scores_turned")
        s_e2 = sem("l2_exponentials")
        s_eh = sem("l2_exponentials_hi")
        s_el = sem("l2_exponentials_lo")
        s_pv = sem("l2_mixed")
        s_ob = sem("l2_mixed_copied")
        s_cx = sem("l2_heads_joined")
        s_ct = sem("l2_joined_turned")
        s_ch = sem("l2_joined_hi")
        s_cl = sem("l2_joined_lo")
        s_wo = sem("l2_out_products")
        s_w8 = sem("fp8_weights_ready")
        s_q5 = sem("fp8_x_ready")
        s_t5 = sem("fp8_x_turned")
        s_c5 = sem("fp8_x_copied")
        s_p5 = sem("fp8_products")
        s_wv = sem("l3_vo_products")
        s_wh = sem("l3_vo_hi")
        s_wl = sem("l3_vo_lo")
        s_lo = sem("lora_products")
        s_la = sem("lora_added")
        s_g3 = sem("l3_gains_joined")
        s_kp = sem("l3_key_products")
        s_kh = sem("l3_key_hi")
        s_kl = sem("l3_key_lo")
        s_k2 = sem("l3_key_squares")
        s_q3 = sem("l3_query_products")
        s_q3h = sem("l3_query_hi")
        s_q3l = sem("l3_query_lo")
        s_q32 = sem("l3_query_squares")
        s_ss = sem("l3_square_sums")
        s_sv = sem("l3_square_sums_scaled")
        s_rs = sem("l3_inverse_rms")
        s_kq = sem("l3_key_parts")
        s_kt = sem("l3_key_parts_turned")
        s_kc = sem("l3_key_parts_copied")
        s_rb = sem("l3_key_rms_spread")
        s_rc = sem("l3_key_rms_copied")
        s_s3 = sem("l3_scores")
        s_m3 = sem("l3_scores_scaled")
        s_b3 = sem("l3_maxima")
        s_e3 = sem("l3_exponentials")
        s_n3 = sem("l3_attention_normalised")
        s_t3 = sem("l3_attention_turned")
        s_th = sem("l3_attention_hi")
        s_tl = sem("l3_attention_lo")
        s_c3 = sem("l3_context_mixed")
        s_oh = sem("l3_mixed_hi")
        s_ol = sem("l3_mixed_lo")
        s_y3 = sem("l3_out_products")
        s_x = [sem(f"x_after_{n}") for n in range(8)]
        s_out = sem("stored")

        def R(i):
            return rt[:, i, :].rearrange("p (t e) -> p t e", t=NT)[:, :, 0:E0]

        def rt8(i):
            return rt[:, i, 0:NT * E3].rearrange("p (t e) -> p t e", t=NT)

        class Order:

            def __init__(self, eng, own):
                self.eng, self.own, self.n = eng, own, {}

            def go(self, ins, sm=None):
                sm = sm or self.own
                ins.then_inc(sm, 1)
                self.n[id(sm)] = self.n.get(id(sm), 0) + 1
                return self.n[id(sm)]

            def do(self, ins, sm=None):
                n = self.go(ins, sm)
                self.eng.wait_ge(sm or self.own, n)

        LOADS = [(w_rt.rearrange("p k e -> p (k e)"), KD * 2 * E0,
                  RWh[:, :, :].rearrange("p k e -> p (k e)"), RWl[:, :, :].rearrange("p k e -> p (k e)"))]
        FF0 = len(LOADS)
        L1W = len(LOADS) + NJ0
        CTX = L1W + 1
        LOADS += [(w_ffn0[:, j, :], CH, W0h[:, j, :], W0l[:, j, :]) for j in range(NJ0)]
        LOADS += [(l1_w, 2 * C, L1Wh[:, :], L1Wl[:, :])]
        LOADS += [(ctx_t[:, 2 * q:2 * q + 2, :].rearrange("p b s -> p (b s)"), 2 * S,
                   CTh[:, 2 * q:2 * q + 2, :].rearrange("p b s -> p (b s)"),
                   CTl[:, 2 * q:2 * q + 2, :].rearrange("p b s -> p (b s)")) for q in range(2)]
        L2W = len(LOADS)
        LOADS += [(w, 2 * D, W2h[:, q, :], W2l[:, q, :]) for q, w in
                  enumerate((l2_q.rearrange("p k n -> p (k n)"), l2_kv, l2_dca,
                             l2_o.rearrange("p k n -> p (k n)")))]
        LOADS += [(ctx[:, 2 * q:2 * q + 2, :, :].rearrange("p b i c -> p (b i c)"), 4 * C,
                   CXTh[:, 2 * q:2 * q + 2, :, :].rearrange("p b i c -> p (b i c)"),
                   CXTl[:, 2 * q:2 * q + 2, :, :].rearrange("p b i c -> p (b i c)")) for q in range(2)]
        LOADS += [(w_r3.rearrange("p k e -> p (k e)"), KD * E3,
                   RV3h[:, :, :].rearrange("p k e -> p (k e)"), RV3l[:, :, :].rearrange("p k e -> p (k e)"))]
        EARLY = len(LOADS)
        CENTRE = 8
        TERNARY = 20
        SAME = (1, I3 // 128)
        NP2 = H2 // 2
        AHEAD = NP2 + 2
        TURN = NP2 - 2

        def bank2(n):
            return 2 * (n % 2) if n < AHEAD else 0

        def maxima_of(n):
            return 4 * n

        NLC = NLORA * I3 // 128
        LOADS += [(w_ffn3[:, j, :], CH, W3h[:, j, :], W3l[:, j, :]) for j in range(NLC)]
        QKW = len(LOADS)
        LOADS += [(l3_k[:, 512 * q:512 * q + 512], 512, W3kh[:, 512 * q:512 * q + 512],
                   W3kl[:, 512 * q:512 * q + 512]) for q in range(4)]
        LOADS += [(l3_q[:, q // 4, 512 * (q % 4):512 * (q % 4) + 512], 512,
                   W3qh[:, q // 4, 512 * (q % 4):512 * (q % 4) + 512],
                   W3ql[:, q // 4, 512 * (q % 4):512 * (q % 4) + 512]) for q in range(8)]
        FF3 = len(LOADS)
        LOADS += [(w_ffn3[:, j, :], CH, W3h[:, j, :], W3l[:, j, :]) for j in range(NLC, NJ3)]
        FRONT = {1: 0, 2: 1, 4: 2, 6: 3, 7: 4}

        block = ctxs.enter_context(nc.Block())

        @block.sync
        def _(sp):
            sp.dma_start(X[:, :, :], x).then_inc(s_in["x"], 16)
            sp.dma_start(idf[:, :], ident).then_inc(s_in["id"], 16)
            sp.dma_start(guT, gu_t).then_inc(s_in["gu"], 16)
            sp.dma_start(ctT, ctx_t).then_inc(s_in["ct"], 16)
            sp.dma_start(iota_b[:, :], iota.partition_broadcast(128)).then_inc(s_in["rt"], 16)
            sp.dma_start(rta[:, :, :].rearrange("p a e -> p (a e)"), rt_aff.partition_broadcast(128))\
              .then_inc(s_in["rt"], 16)
            sp.dma_start(b1[:, :], l1_b).then_inc(s_in["rt"], 16)

            def load(n):
                src, w, _, _ = LOADS[n]
                if n >= RING:
                    sp.wait_ge(s_w, n - RING + 1)
                sp.dma_start(ring[:, n % RING, 0:w], src).then_inc(s_ring[n % RING], 16)

            for n in range(EARLY):
                load(n)
            sp.wait_ge(s_x[0], B)
            sp.dma_start(rawU, w_up.rearrange("p k n -> p (k n)")).then_inc(s_in["tw"], 16)
            sp.dma_start(rawD, w_dn.rearrange("p k n -> p (k n)")).then_inc(s_in["tw"], 16)
            sp.wait_ge(s_x[2], B)
            a = 0
            parts = {}
            for name, n in (("bq", D), ("bo", D), ("qw", 16), ("qb", 16), ("kw", 16), ("kb", 16),
                            ("dw", 16), ("db", 16), ("bkv", 2 * D), ("bd", 2 * D)):
                parts[name] = l2_aff[a:a + n]
                a += n
            for dst, name in ((BQO[:, 0, :], "bq"), (BQO[:, 1, :], "bo"), (QG2[:, 0, :], "qw"),
                              (QG2[:, 1, :], "qb"), (KG2[:, 0, 0, :], "kw"), (KG2[:, 0, 1, :], "kb"),
                              (KG2[0:128 - DCA, 1, 0, :], "kw"), (KG2[0:128 - DCA, 1, 1, :], "kb"),
                              (KG2[128 - DCA:128, 1, 0, :], "dw"), (KG2[128 - DCA:128, 1, 1, :], "db"),
                              (BKV[:, 0, :], "bkv"), (BKV[0:128 - DCA, 1, :], "bkv"),
                              (BKV[128 - DCA:128, 1, :], "bd")):
                sp.dma_start(dst, parts[name].partition_broadcast(dst.shape[0])).then_inc(s_in["l2"], 16)
            sp.dma_start(mask[:, :, :], masks).then_inc(s_in["l2"], 16)
            sp.dma_start(v5[:, 0:1], w8_sc.partition_broadcast(128)).then_inc(s_in["w8"], 16)
            sp.dma_start(v5b[:, 0:1], in_sc.partition_broadcast(128)).then_inc(s_in["w8"], 16)
            sp.wait_ge(s_x[4], B)
            sp.dma_start(w8r, w8.rearrange("p k n -> p (k n)")).then_inc(s_in["w8"], 16)
            sp.dma_start(g3[:, 0:2], l3_g).then_inc(s_in["g3"], 16)
            sp.dma_start(tmp3[:, 0:1], temp.partition_broadcast(128)).then_inc(s_in["g3"], 16)
            sp.wait_ge(s_x[4], B)
            for dst, src in ((rawV, l3_v), (rawO, l3_o)):
                sp.dma_start(dst, src).then_inc(s_in["vo"], 16)
            for dst, src in ((LA3, lo_a), (LB3, lo_b), (LD3, lo_da), (LE3, lo_db)):
                sp.dma_start(dst[0:RANK], src).then_inc(s_in["lo"], 16)
            for n in range(EARLY, len(LOADS)):
                load(n)
            for b in range(B):
                sp.wait_ge(s_x[7], b + 1)
                sp.dma_start(out[:, 2 * b:2 * b + 2, :], X[:, 2 * b:2 * b + 2, :]).then_inc(s_out, 16)
            sp.wait_ge(s_out, 16 * B)

        @block.gpsimd
        def _(pool):
            P = Order(pool, s_pool)
            P.go(pool.memset(onesf[:, :], 1.0), s_cst)
            P.go(pool.memset(magic[:, :], MAGIC), s_cst)
            pool.wait_ge(s_in["id"], 16)
            P.go(pool.tensor_copy(idb[:, :], idf[:, :]), s_cst)
            P.go(pool.tensor_copy(idh[:, :], idf[:, :]), s_cst)
            pool.dma_start(sel0b[:, :], sel0).then_inc(s_sel, 16)
            pool.dma_start(sel3b[:, :], sel3).then_inc(s_sel, 16)
            pool.dma_start(SR3[:, :], selr).then_inc(s_sel, 16)
            P.go(pool.memset(half[:, :], -0.5), s_cst)

            def split(n):
                _, w, hi, lo = LOADS[n]
                pool.wait_ge(s_ring[n % RING], 16 * (n // RING + 1))
                if EARLY <= n < QKW:
                    pool.wait_ge(s_la, n - EARLY + 1)
                if n == FF3:
                    pool.wait_ge(s_wl, H3 // 2)
                if n == L2W:
                    pool.wait_ge(s_x[0], B)
                if L2W <= n < L2W + 3:
                    pool.wait_ge(s_lc, n - L2W + 1)
                if QKW <= n < FF3:
                    pool.wait_ge(s_hi, n - QKW + 1)
                else:
                    P.do(pool.tensor_copy(hi, ring[:, n % RING, 0:w]))
                P.go(pool.tensor_tensor(lo, ring[:, n % RING, 0:w], hi, ALU.subtract), s_w)

            for n in range(EARLY):
                split(n)
            pool.wait_ge(s_w, EARLY)
            pool.wait_ge(s_x[1], B)
            for q, v in ((0, CMh), (1, CMl)):
                src = (CTh, CTl)[q]
                P.go(pool.memset(v[:, :, 0, 128 - DCA:128], 0.0), s_cm2)
                P.go(pool.memset(v[:, :, 1, 0:128 - DCA], 0.0), s_cm2)
                P.go(pool.tensor_copy(v[:, :, 0, 0:128 - DCA], src[:, :, 128:S - DCA]), s_cm2)
                P.go(pool.tensor_copy(v[:, :, 1, 128 - DCA:128], src[:, :, S - DCA:S]), s_cm2)
            pool.wait_ge(s_x[2], B)
            P.go(pool.memset(HS2[:, :, :, :, 48:64], 0.0), s_z2)
            pool.wait_ge(s_in["l2"], 16 * 14)
            pool.wait_ge(s_z2, 1)
            for kt in range(2):
                for q in range(2):
                    P.go(pool.tensor_copy(HS2[:, :, kt, :, 48 + q], mask[:, kt, q:q + 1].unsqueeze(2)
                                          .broadcast_to([128, B, H2])), s_z2)
            pool.wait_ge(s_x[3], B)
            for v in (VEh[:, 0, :, :, 17:34], VEl[:, 0, :, :, 16:34], VEl[:, 1, :, :, 16:34:17]):
                P.go(pool.memset(v, 0.0), s_z2)
            pool.wait_ge(s_in["l2"], 16 * 14)
            pool.wait_ge(s_z2, 8)
            for kt in range(2):
                for part in range(kt + 1):
                    P.go(pool.tensor_copy(VEh[:, kt, :, :, 17 * part + 16],
                                          mask[:, kt, part:part + 1].unsqueeze(2).broadcast_to([128, B, H2])),
                         s_z2)
            pool.wait_ge(s_vh, 1)
            P.go(pool.tensor_tensor(VEl[:, 0, :, :, 0:16].rearrange("p b h r -> p (b h) r"),
                                    VF[:, 0, :, :].rearrange("p b (h r) -> p (b h) r", h=H2),
                                    VEh[:, 0, :, :, 0:16].rearrange("p b h r -> p (b h) r"),
                                    ALU.subtract))
            for g in range(B * H2):
                pool.wait_ge(s_eh, g + 1)
                if g >= 4:
                    pool.wait_ge(s_pv, g - 3)
                P.go(pool.tensor_tensor(El2[:, g % 4, :], EX2[:, g % 4, :], Eh2[:, g % 4, :],
                                        ALU.subtract), s_el)
            pool.wait_ge(s_x[4], B)
            for n in range(EARLY, FF3):
                split(n)
            pool.wait_ge(s_cst, 5)
            for G in range(NG):
                pool.wait_ge(s_sv, 2 * G + 1)
                k, q = (rs3[:, G % 2, w, :, :].rearrange("p i h -> p (i h)") for w in range(2))
                P.do(pool.tensor_tensor(k, k, half[:, :].broadcast_to([128, 2 * HG]), ALU.pow))
                k = rs3[:, G % 2, 0, :, :]
                if G >= 1:
                    pool.wait_ge(s_kt, G)
                t = kt3[:, :, :]
                P.do(pool.tensor_copy(KP3[:, :, 0:HG], k))
                P.do(pool.tensor_tensor(t, k, KP3[:, :, 0:HG], ALU.subtract))
                P.do(pool.tensor_copy(KP3[:, :, HG:2 * HG], t))
                P.go(pool.tensor_tensor(KP3[:, :, 2 * HG:3 * HG], t, KP3[:, :, HG:2 * HG],
                                        ALU.subtract), s_kq)
                pool.wait_ge(s_sv, 2 * G + 2)
                P.go(pool.tensor_tensor(q, q, half[:, :].broadcast_to([128, 2 * HG]), ALU.pow), s_rs)
                n = FF3 + G
                if n < len(LOADS):
                    split(n)

        @block.tensor
        def _(pe):
            def sq_turn(n, b):
                kc = 2 - n
                if n == 0:
                    pe.wait_ge(s_ln, b + 1)
                    src = XN[:, 2 * b:2 * b + 2, :]
                else:
                    pe.wait_ge(s_ha, b + 1)
                    src = HA[:, b, :, :]
                for k in range(kc):
                    for i in range(2):
                        t = pe.transpose(PS[2 * b][:, k * S + 128 * i:k * S + 128 * i + 128],
                                         src[:, i, 128 * k:128 * k + 128], idf[:, :])
                t.then_inc(s_xt, 1)

            def sq_back(n, b):
                kc, w = 2 - n, 128 * (2 - n)
                pe.wait_ge(s_xs, 4 * n + b + 1)
                for k in range(kc):
                    for i in range(2):
                        pe.transpose(PS[2 * b][:, i * w + 128 * k:i * w + 128 * k + 128],
                                     QS[:, b, k, 128 * i:128 * i + 128], idf[:, :])
                pe.wait_ge(s_ws, 4 * n + b + 1)
                for k in range(kc):
                    for i in range(2):
                        t = pe.transpose(PS[2 * b + 1][:, i * w + 128 * k:i * w + 128 * k + 128],
                                         QS[:, b, 2 + k, 128 * i:128 * i + 128], idf[:, :])
                t.then_inc(s_bk, 1)

            def sq_ints(n, b):
                kc = 2 - n
                pe.wait_ge(s_qb, 4 * n + b + 1)
                dst = PS[2 * b][:, :].bitcast(bf16)
                for j in range(4):
                    for k in range(kc):
                        at = ((j // 2) * kc + k) * S + (j % 2) * 128
                        t = pe.transpose(dst[:, at:at + 128], QB[:, b, j, 128 * k:128 * k + 128], idb[:, :])
                t.then_inc(s_qt, 1)

            def sq_mul(n, b):
                kc = 2 - n
                pe.wait_ge(s_qc, 4 * n + b + 1)
                pe.wait_ge(s_dg, 4 * n + b + 1)
                for i in range(2):
                    for k in range(kc):
                        pe.matmul(PS[2 * b + 1][:, i * S:i * S + S], QTt[:, b, k, 128 * i:128 * i + 128],
                                  QTt[:, b, kc + k, :], start=(k == 0), stop=(k == kc - 1))
                for i in range(2):
                    t = pe.matmul(PS[2 * b][:, 128 * i:128 * i + 128], onesf[:, :], DG[:, b, i, :],
                                  start=True, stop=True)
                t.then_inc(s_pr, 1)

            def front(part, b, bank):
                if part == 2:
                    pe.wait_ge(s_at, b + 1)
                pe.wait_ge(s_ln, 4 * part + b + 1)
                for k in range(KD):
                    for i in range(2):
                        t = pe.transpose(PS[bank][:, k * S + 128 * i:k * S + 128 * i + 128],
                                         XN[:, 2 * b + i, 128 * k:128 * k + 128], idf[:, :])
                t.then_inc(s_ft, 1)

            def router0():
                pe.wait_ge(s_w, 1)
                for t in range(NT):
                    if t % 2 == 0:
                        pe.wait_ge(s_xh, t // 2 + 1)
                        pe.wait_ge(s_xl, t // 2 + 1)
                    o = PS[7][:, 2 * E0 * t:2 * E0 * (t + 1)]
                    for k in range(KD):
                        xh, xl = (v[:, k, 128 * t:128 * t + 128] for v in (XTh, XTl))
                        pe.matmul(o, xh, RWh[:, k, :], start=(k == 0), stop=False)
                        pe.matmul(o, xh, RWl[:, k, :], start=False, stop=False)
                        m = pe.matmul(o, xl, RWh[:, k, :], start=False, stop=(k == KD - 1))
                m.then_inc(s_rp, 1)

            def turn_combine(layer, rows):
                pe.wait_ge(s_cm, layer + 1)
                for t in range(NT):
                    m = pe.transpose(PS[7][0:rows, :].bitcast(bf16)[:, 128 * t:128 * t + 128],
                                     CM[:, t, 0:rows], idb[:, :])
                m.then_inc(s_cw, 1)

            def ternary_sums():
                pe.wait_ge(s_pa, 1)
                pe.matmul(PS[7][:, 0:2], onesf[:, :], v1[:, 0:2], start=True, stop=True).then_inc(s_ps, 1)

            def ffn(layer, Wh, Wl, nj, sel, rows, first, turn):
                base = layer * 2 * NJ0
                units = [(h, j) for h in range(2) for j in range(nj)]

                def gate_up(n):
                    h, j = units[n]
                    if h == 0:
                        pe.wait_ge(s_w, first + j + 1)
                    if n >= 2:
                        pe.wait_ge(s_t1, base + n - 1)
                    for part in range(2):
                        o = PS[2 + 2 * (n % 2) + part][:, :]
                        for k in range(KD):
                            c = 2 * 128 * part + 128 * k
                            xh, xl = (v[:, k, 512 * h:512 * h + 512] for v in (XTh, XTl))
                            pe.matmul(o, Wh[:, j, c:c + 128], xh, start=(k == 0), stop=False)
                            pe.matmul(o, Wh[:, j, c:c + 128], xl, start=False, stop=False)
                            m = pe.matmul(o, Wl[:, j, c:c + 128], xh, start=False, stop=(k == KD - 1))
                    m.then_inc(s_gu, 1)

                def combine(n):
                    h, j = units[n]
                    if n >= 1:
                        pe.wait_ge(s_t2, base + n)
                    pe.matmul(PS[6][:, :], sel[:, 128 * j:128 * j + 128], combT[0:rows, 512 * h:512 * h + 512],
                              start=True, stop=True).then_inc(s_cb, 1)

                def down(n):
                    h, j = units[n]
                    pe.wait_ge(s_hh, base + n + 1)
                    pe.wait_ge(s_hl, base + n + 1)
                    if j == 0 and h == 1:
                        pe.wait_ge(s_x[1 if layer == 0 else 7], 2)
                    for i in range(4):
                        o = PS[i // 2][:, (i % 2) * D:(i % 2) * D + D]
                        hh, hl = (v[:, n % 2, 128 * i:128 * i + 128] for v in (Hh, Hl))
                        wh, wl = (v[:, j, 512:512 + D] for v in (Wh, Wl))
                        pe.matmul(o, hh, wh, start=(j == 0 and i % 2 == 0), stop=False, skip_group_check=True)
                        pe.matmul(o, hh, wl, start=False, stop=False, skip_group_check=True)
                        m = pe.matmul(o, hl, wh, start=False, stop=(j == nj - 1), skip_group_check=True)
                    m.then_inc(s_dn, 1)

                for n in range(len(units) + 2):
                    if n < len(units):
                        gate_up(n)
                    if n == 1:
                        turn()
                        pe.wait_ge(s_cT, layer + 1)
                        pe.wait_ge(s_sel, 48)
                    if 1 <= n <= len(units) and (n - 1) % SAME[layer] == 0:
                        combine(n - 1)
                    if layer == 0 and n == TERNARY + 1:
                        ternary_sums()
                    if n >= 2:
                        down(n - 2)

            pe.wait_ge(s_cst, 4)
            for n in range(2):
                for step in (sq_turn, sq_back, sq_ints, sq_mul):
                    for b in range(B):
                        step(n, b)
            for b in range(B):
                front(1, b, 2 * b)
            router0()
            ffn(0, W0h, W0l, NJ0, sel0b, K0, FF0, lambda: turn_combine(0, K0))

            def three(o, lh, ll, rh, rl, first=True, last=True):
                pe.matmul(o, lh, rh, start=first, stop=False)
                pe.matmul(o, lh, rl, start=False, stop=False)
                return pe.matmul(o, ll, rh, start=False, stop=last)

            def l1_query_key(b):
                for q in range(2):
                    m = three(PS[2 * b][:, q * S:q * S + S], L1Wh[:, q * C:q * C + C], L1Wl[:, q * C:q * C + C],
                              CTh[:, b, :], CTl[:, b, :])
                m.then_inc(s_qk, 1)

            def l1_energy(b):
                pe.wait_ge(s_qh, b + 1)
                pe.wait_ge(s_ql, b + 1)
                for i in range(2):
                    m = three(PS[2 * b + 1][:, i * S:i * S + S], QK1h[:, b, 0, 128 * i:128 * i + 128],
                              QK1l[:, b, 0, 128 * i:128 * i + 128], QK1h[:, b, 1, :], QK1l[:, b, 1, :])
                m.then_inc(s_en, 1)

            def l1_turn(b):
                pe.wait_ge(s_an, b + 1)
                for k in range(2):
                    for i in range(2):
                        m = pe.transpose(PS[2 * b][:, k * S + 128 * i:k * S + 128 * i + 128],
                                         EX1[:, b, i, 128 * k:128 * k + 128], idf[:, :])
                m.then_inc(s_tt, 1)

            def l1_mix(b):
                f = 4 * FRONT[2] + b + 1
                pe.wait_ge(s_xh, f)
                pe.wait_ge(s_xl, f)
                pe.wait_ge(s_at, b + 1)
                for i in range(2):
                    t = 128 * (2 * b + i)
                    for k in range(KD):
                        m = three(PS[2 * b + 1][:, i * S:i * S + S], XTh[:, k, t:t + 128], XTl[:, k, t:t + 128],
                                  AT1h[:, b, k, :], AT1l[:, b, k, :], k == 0, k == 1)
                m.then_inc(s_xm, 1)

            def l1_turn_x(b):
                pe.wait_ge(s_q8, b + 1)
                for k in range(KD):
                    for i in range(2):
                        at = k * S + 128 * i
                        m = pe.transpose(PS[2 * b][:, :].bitcast(bf16)[:, at:at + 128],
                                         XQ1[:, b, i, 128 * k:128 * k + 128], idb[:, :])
                m.then_inc(s_qT, 1)

            def l1_up(b):
                pe.wait_ge(s_q9, b + 1)
                pe.wait_ge(s_tw, 2)
                for i in range(2):
                    for k in range(KD):
                        m = pe.matmul(PS[2 * b + i][:, :], XQT1[:, b, k, 128 * i:128 * i + 128], TWu[:, k, :],
                                      start=(k == 0), stop=(k == KD - 1))
                m.then_inc(s_up, 1)

            def l1_turn_h(b):
                pe.wait_ge(s_h8, b + 1)
                for c in range(4):
                    for i in range(2):
                        at = c * S + 128 * i
                        m = pe.transpose(PS[2 * b][:, :].bitcast(bf16)[:, at:at + 128],
                                         HQ1[:, b, i, 128 * c:128 * c + 128], idb[:, :])
                m.then_inc(s_hT, 1)

            def l1_down(b):
                pe.wait_ge(s_h9, b + 1)
                for i in range(2):
                    for c in range(4):
                        m = pe.matmul(PS[2 * b + 1][:, i * D:i * D + D], HT1[:, b, c, 128 * i:128 * i + 128],
                                      TWd[:, c, :], start=(c == 0), stop=(c == 3))
                m.then_inc(s_d1, 1)

            pe.wait_ge(s_w, CTX + 2)
            pe.wait_ge(s_x[1], B)
            for step in (l1_query_key, l1_energy, l1_turn, lambda b: front(2, b, 2 * b), l1_mix):
                for b in range(B):
                    step(b)
            pe.wait_ge(s_x[2], B)
            for step in (l1_turn_x, l1_up, l1_turn_h, l1_down):
                for b in range(B):
                    step(b)

            def l2_turn_heads(n):
                b = n % B
                pe.wait_ge(s_k3, n // 2 + 1)
                for hp in range(H2 // 2):
                    for i in range(2):
                        at = (hp % 4) * S + 128 * i
                        m = pe.transpose(PS[2 * b + hp // 4][:, :].bitcast(f16)[:, at:at + 128],
                                         HS2[:, b, i, 2 * hp:2 * hp + 2, :].rearrange("p h r -> p (h r)"),
                                         idh[:, :])
                m.then_inc(s_k4, 1)

            def l2_keys_values(b):
                p0, p1 = PS[2 * b][:, :], PS[2 * b + 1][:, :]
                three(p0, CTh[:, b, 0:128], CTl[:, b, 0:128], W2h[:, 1, :], W2l[:, 1, :])
                three(p1, CMh[:, b, 0, :], CMl[:, b, 0, :], W2h[:, 1, :], W2l[:, 1, :], True, False)
                three(p1, CMh[:, b, 1, :], CMl[:, b, 1, :], W2h[:, 2, :], W2l[:, 2, :], False, True)\
                    .then_inc(s_kv, 1)

            def l2_query(b):
                f = 4 * FRONT[4] + b + 1
                pe.wait_ge(s_xh, f)
                pe.wait_ge(s_xl, f)
                for i in range(2):
                    t = 128 * (2 * b + i)
                    for k in range(KD):
                        m = three(PS[2 * b + 1][:, i * D:i * D + D], XTh[:, k, t:t + 128], XTl[:, k, t:t + 128],
                                  W2h[:, 0, k * D:k * D + D], W2l[:, 0, k * D:k * D + D], k == 0, k == 1)
                m.then_inc(s_qp, 1)

            def l2_score(b, p):
                n = NP2 * b + p
                free = n if n >= AHEAD else n - 1
                if free > 0:
                    pe.wait_ge(s_m2, maxima_of(free))
                if p == 0 or n == 1:
                    pe.wait_ge(s_k5, 2 * (B + b + p + 1))
                for i in range(2):
                    for q in range(2):
                        r = 64 * q
                        m = pe.matmul(PS[bank2(n) + q][:, i * S:i * S + S], QT3[r:r + 64, b, p, 128 * i:128 * i + 128],
                                      KT3[r:r + 64, b, p, :], start=True, stop=True)
                m.then_inc(s_s2, 1)

            def l2_turn_maxima(b):
                pe.wait_ge(s_m2, maxima_of(NP2 * (b + 1)))
                for hp in range(H2 // 2):
                    for i in range(2):
                        at = (hp % 4) * S + 128 * i
                        m = pe.transpose(PS[6 + hp // 4][:, :].bitcast(f16)[:, at:at + 128],
                                         HS2[:, b, i, 2 * hp:2 * hp + 2, :].rearrange("p h r -> p (h r)"),
                                         idh[:, :])
                m.then_inc(s_mt, 1)

            def l2_score_turned(b, p):
                if p == 0:
                    pe.wait_ge(s_mc, b + 1)
                if b + p > 0:
                    pe.wait_ge(s_e2, H2 * b + 2 * p)
                else:
                    pe.wait_ge(s_m2, maxima_of(AHEAD))
                for kt in range(2):
                    for q in range(2):
                        r = 64 * q
                        m = pe.matmul(PS[2 + q][:, kt * S:kt * S + S], KT3[r:r + 64, b, p, 128 * kt:128 * kt + 128],
                                      QT3[r:r + 64, b, p, :], start=True, stop=True)
                m.then_inc(s_st, 1)

            def l2_values(g):
                b, h = g // H2, g % H2
                pe.wait_ge(s_eh, g + 1)
                pe.wait_ge(s_el, g + 1)
                if h % 4 == 0 and g >= 8:
                    pe.wait_ge(s_ob, g // 4 - 1)
                for i in range(2):
                    o = PS[4 + (g // 4) % 2][:, (4 * i + h % 4) * VE:(4 * i + h % 4 + 1) * VE]
                    for kt in range(2):
                        at = kt * S + 128 * i
                        m = three(o, Eh2[:, g % 4, at:at + 128], El2[:, g % 4, at:at + 128],
                                  VEh[:, kt, b, h, :], VEl[:, kt, b, h, :], kt == 0, kt == 1)
                m.then_inc(s_pv, 1)

            def l2_turn_joined(b):
                pe.wait_ge(s_cx, b + 1)
                for k in range(KD):
                    for i in range(2):
                        m = pe.transpose(PS[7][:, k * S + 128 * i:k * S + 128 * i + 128],
                                         CX2[:, i, 128 * k:128 * k + 128], idf[:, :])
                m.then_inc(s_ct, 1)

            def l2_out(b):
                pe.wait_ge(s_ch, b + 1)
                pe.wait_ge(s_cl, b + 1)
                for i in range(2):
                    for k in range(KD):
                        m = three(PS[6][:, i * D:i * D + D], CXh[:, k, 128 * i:128 * i + 128],
                                  CXl[:, k, 128 * i:128 * i + 128], W2h[:, 3, k * D:k * D + D],
                                  W2l[:, 3, k * D:k * D + D], k == 0, k == 1)
                m.then_inc(s_wo, 1)

            def fp8_turn(b):
                pe.wait_ge(s_q5, b + 1)
                for k in range(KD):
                    for i in range(2):
                        at = k * S + 128 * i
                        m = pe.transpose(PS[2 * b][:, :].bitcast(bf16)[:, at:at + 128],
                                         Q5[:, b, i, 128 * k:128 * k + 128], idb[:, :])
                m.then_inc(s_t5, 1)

            def fp8_mul(b):
                pe.wait_ge(s_c5, b + 1)
                pe.wait_ge(s_w8, 1)
                for i in range(2):
                    for k in range(KD):
                        m = pe.matmul(PS[2 * b + 1][:, i * D:i * D + D], QT5[:, b, k, 128 * i:128 * i + 128],
                                      W8[:, k * D:k * D + D], start=(k == 0), stop=(k == 1))
                m.then_inc(s_p5, 1)

            pe.wait_ge(s_x[3], B)
            pe.wait_ge(s_cm2, 8)
            for b in range(B):
                l2_keys_values(b)
            for b in range(B):
                l2_turn_heads(b)
            for b in range(B):
                pe.wait_ge(s_k5, 2 * (b + 1))
                front(4, b, 2 * b)
            for b in range(B):
                l2_query(b)
            for b in range(B):
                l2_turn_heads(B + b)
            for n in range(AHEAD):
                if n == NP2:
                    pe.wait_ge(s_k5, 4 * B)
                    l2_turn_maxima(0)
                l2_score(n // NP2, n % NP2)
            for k in range(B * NP2 + 5):
                b, p = k // NP2, k % NP2
                if b < B:
                    l2_score_turned(b, p)
                if p == TURN and b + 1 < B:
                    if b >= 1:
                        pe.wait_ge(s_x[4], b)
                    l2_turn_maxima(b + 1)
                if k + AHEAD < B * NP2:
                    l2_score((k + AHEAD) // NP2, (k + AHEAD) % NP2)
                if 1 <= k <= B * NP2:
                    l2_values(2 * k - 2)
                    l2_values(2 * k - 1)
                if b >= 1 and p == 3:
                    l2_turn_joined(b - 1)
                if b >= 1 and p == 4:
                    l2_out(b - 1)

            def l3_vo(n):
                for q in range(2):
                    m = pe.matmul(PS[n][:, q * D:q * D + D], rawV[:, 2 * n + q, :], rawO[:, 2 * n + q, :],
                                  start=True, stop=True)
                m.then_inc(s_wv, 1)

            def lora(c):
                e, f = c // (I3 // 128), 128 * (c % (I3 // 128))
                for q in range(2):
                    for k in range(KD):
                        at = q * D + 128 * k
                        pe.matmul(PS[2 * c][:, at:at + 128], LA3[0:RANK, e, q, 128 * k:128 * k + 128],
                                  LB3[0:RANK, e, q, f:f + 128], start=True, stop=True)
                pe.matmul(PS[2 * c + 1][:, 0:D], LD3[0:RANK, e, f:f + 128], LE3[0:RANK, e, :],
                          start=True, stop=True).then_inc(s_lo, 1)

            def l3_keys(G, q):
                b, h = G // HG, HG * (G % HG) + 2 * q
                n = 2 * G + q
                if n >= 1:
                    pe.wait_ge(s_q3h, 2 * G - 1 if q == 0 else 2 * G)
                    pe.wait_ge(s_q3l, 2 * G - 1 if q == 0 else 2 * G)
                    pe.wait_ge(s_q32, 2 * G - 1 if q == 0 else 2 * G)
                for i in range(2):
                    c = (h + i) * HD3
                    m = three(PS[1 + q][:, i * S:i * S + S], W3kh[:, c:c + 128], W3kl[:, c:c + 128],
                              CTh[:, b, :], CTl[:, b, :])
                m.then_inc(s_kp, 1)

            def l3_queries(G, q):
                b, h = G // HG, HG * (G % HG) + 2 * q
                for w in (s_kh, s_kl, s_k2):
                    pe.wait_ge(w, 2 * G + q + 1)
                for i in range(2):
                    c = (h + i) * HD3
                    for k in range(KD):
                        m = three(PS[1 + q][:, i * S:i * S + S], W3qh[:, k, c:c + 128], W3ql[:, k, c:c + 128],
                                  XTh[:, k, S * b:S * b + S], XTl[:, k, S * b:S * b + S], k == 0, k == 1)
                m.then_inc(s_q3, 1)

            def l3_sums(G, kq, i):
                if i == 0:
                    pe.wait_ge((s_k2, s_q32)[kq], 2 * G + 2)
                    if kq == 1:
                        pe.wait_ge(s_sv, 2 * G + 1)
                    elif G >= 1:
                        pe.wait_ge(s_rc, 2 * G)
                for h in range(HG):
                    c = (kq * 2 + i) * HG + h
                    at = (h % 2) * S + 128 * i
                    m = pe.matmul(PS[7][:, c:c + 1], SQ3[:, kq, h // 2, at:at + 128], onesf[:, 0:1],
                                  start=True, stop=True)
                if i == 1:
                    m.then_inc(s_ss, 1)

            def l3_turn_rms(G):
                pe.wait_ge(s_kq, G + 1)
                pe.wait_ge(s_sv, 2 * G + 2)
                for i in range(2):
                    m = pe.transpose(PS[7][0:3 * HG, 64:192].bitcast(bf16)[:, 128 * i:128 * i + 128],
                                     KP3[:, i, :], idb[:, :])
                m.then_inc(s_kt, 1)

            def l3_spread_rms(G, q):
                if q == 0:
                    pe.wait_ge(s_kc, G + 1)
                else:
                    pe.wait_ge(s_rc, 2 * G + 1)
                for i in range(2):
                    h = 2 * q + i
                    m = pe.matmul(PS[7][:, i * S:i * S + S], SR3[:, 128 * h:128 * h + 128], KR3[:, :],
                                  start=True, stop=True)
                m.then_inc(s_rb, 1)

            def l3_make(G, j):
                if j < 2:
                    for q in range(2):
                        (l3_keys, l3_queries)[j](G, q)

            def l3_score(n):
                G, h = n // HG, n % HG
                if n >= 2:
                    pe.wait_ge(s_m3, 2 * (n - 1))
                for w in (s_kh, s_kl, s_q3h, s_q3l):
                    pe.wait_ge(w, 2 * G + h // 2 + 1)
                for i in range(2):
                    m = three(PS[3 + n % 2][:, i * S:i * S + S], QG3h[:, G % 2, h, 128 * i:128 * i + 128],
                              QG3l[:, G % 2, h, 128 * i:128 * i + 128], KG3h[:, G % 2, h, :], KG3l[:, G % 2, h, :])
                m.then_inc(s_s3, 1)

            def l3_turn(n):
                pe.wait_ge(s_n3, n + 1)
                if n >= 1:
                    pe.wait_ge(s_th, n)
                    pe.wait_ge(s_tl, n)
                for k in range(2):
                    for i in range(2):
                        m = pe.transpose(PS[5][:, k * S + 128 * i:k * S + 128 * i + 128],
                                         SP3[:, n % 2, i, 128 * k:128 * k + 128], idf[:, :])
                m.then_inc(s_t3, 1)

            def l3_mix(n):
                b = n // H3
                pe.wait_ge(s_th, n + 1)
                pe.wait_ge(s_tl, n + 1)
                if n >= 1:
                    pe.wait_ge(s_oh, n)
                    pe.wait_ge(s_ol, n)
                for k in range(2):
                    m = three(PS[6][:, 0:S], CXTh[:, b, k, :], CXTl[:, b, k, :], PT3h[:, n % 2, k, :],
                              PT3l[:, n % 2, k, :], k == 0, k == 1)
                m.then_inc(s_c3, 1)

            def l3_out(n):
                b, h = n // H3, n % H3
                pe.wait_ge(s_oh, n + 1)
                pe.wait_ge(s_ol, n + 1)
                if h == 0 and b >= 1:
                    pe.wait_ge(s_x[6], b)
                for i in range(2):
                    o = PS[0][:, i * D:i * D + D]
                    oh, ol = (v[:, n % 2, 128 * i:128 * i + 128] for v in (OT3h, OT3l))
                    pe.matmul(o, oh, WVh[:, h, :], start=(h == 0 and i == 0), stop=False, skip_group_check=True)
                    pe.matmul(o, oh, WVl[:, h, :], start=False, stop=False, skip_group_check=True)
                    m = pe.matmul(o, ol, WVh[:, h, :], start=False, stop=(h == H3 - 1), skip_group_check=True)
                m.then_inc(s_y3, 1)

            def router3():
                pe.wait_ge(s_w, EARLY)
                for t in range(NT):
                    o = PS[7][:, E3 * t:E3 * (t + 1)]
                    for k in range(KD):
                        m = three(o, XTh[:, k, 128 * t:128 * t + 128], XTl[:, k, 128 * t:128 * t + 128],
                                  RV3h[:, k, :], RV3l[:, k, :], k == 0, k == 1)
                m.then_inc(s_rp, 1)

            pe.wait_ge(s_x[4], B)
            pe.wait_ge(s_in["vo"], 32)
            for n in range(H3 // 2):
                l3_vo(n)
            pe.wait_ge(s_wh, H3 // 2)
            pe.wait_ge(s_wl, H3 // 2)
            pe.wait_ge(s_in["lo"], 64)
            for c in range(NLC):
                lora(c)
            pe.wait_ge(s_la, NLC)
            pe.wait_ge(s_x[4], B)
            for step in (fp8_turn, fp8_mul):
                for b in range(B):
                    step(b)
            pe.wait_ge(s_x[5], B)
            for b in range(B):
                front(6, b, 2 * b)
            pe.wait_ge(s_xh, 4 * FRONT[6] + B)
            pe.wait_ge(s_xl, 4 * FRONT[6] + B)
            pe.wait_ge(s_w, FF3)
            for j in range(2):
                l3_make(0, j)
            for kq in range(2):
                for i in range(2):
                    l3_sums(0, kq, i)
            l3_turn_rms(0)
            for q in range(2):
                l3_spread_rms(0, q)
            N3 = B * H3
            for n in range(-1, N3 + 5):
                G, j = n // HG + 1, n % HG
                some = 0 <= n and G < NG
                if n + 1 < N3:
                    l3_score(n + 1)
                if some and j in (1, 2):
                    l3_sums(G, j - 1, 0)
                elif some and j == 3:
                    l3_turn_rms(G)
                if n >= 5:
                    l3_out(n - 5)
                if some and j == 3:
                    l3_spread_rms(G, 0)
                if 3 <= n < N3 + 3:
                    l3_mix(n - 3)
                if some and j in (1, 2):
                    l3_sums(G, j - 1, 1)
                elif some and j == 3:
                    l3_spread_rms(G, 1)
                if 1 <= n <= N3:
                    l3_turn(n - 1)
                if (n + 1) // HG + 1 < NG:
                    l3_make((n + 1) // HG + 1, (n + 1) % HG)
            pe.wait_ge(s_x[6], B)
            for b in range(B):
                front(7, b, 2 * b)
            pe.wait_ge(s_xh, 4 * FRONT[7] + B)
            pe.wait_ge(s_xl, 4 * FRONT[7] + B)
            router3()
            ffn(1, W3h, W3l, NJ3, sel3b, K3, FF3 - NLC, lambda: turn_combine(1, K3))

        @block.scalar
        def _(act):
            A = Order(act, s_act)
            act.wait_ge(s_cst, 4)
            A.go(act.activation(tmpa[:, 0:1], magic[:, 0:1], ACT.Copy))

            def sq_scale(n, b):
                act.wait_ge(s_iv, 2 * n + 1)
                for k in range(2 - n):
                    m = A.go(act.activation(QS[:, b, k, :], PS[2 * b][:, k * S:k * S + S], ACT.Copy,
                                            scale=sq[:, b, 8 + k:9 + k]), s_xs if k == 1 - n else None)

            def sq_round(n, b):
                w = 128 * (2 - n)
                act.wait_ge(s_iv, 2 * n + 2)
                for j in range(4):
                    A.go(act.activation(QS[:, b, j, 0:w], PS[2 * b + j // 2][:, (j % 2) * w:(j % 2) * w + w],
                                        ACT.Identity, bias=magic[:, 0:1], scale=sq[:, b, 16 + j:17 + j]),
                         s_rd if j == 3 else None)

            def sq_copy(n, b):
                kc = 2 - n
                act.wait_ge(s_qt, 4 * n + b + 1)
                A.go(act.activation(QTt[:, b, 0:2 * kc, :], PS[2 * b][:, :].bitcast(bf16)[:, 0:2 * kc * S],
                                    ACT.Copy), s_qc)

            def sq_spread(n, b):
                act.wait_ge(s_pr, 4 * n + b + 1)
                A.go(act.activation(WB[:, b, :], PS[2 * b][:, 0:S], ACT.Copy), s_wb)

            def gate(b):
                act.wait_ge(s_hu, b + 1)
                A.go(act.activation(HA[:, b, :, :], HU[:, b, :, 0:128], ACT.Silu), s_sl)

            for n in range(2):
                for step in (sq_scale, sq_round, sq_copy, sq_spread):
                    for b in range(B):
                        step(n, b)
                if n == 0:
                    for b in range(B):
                        gate(b)

            def front_hi(part, b, bank):
                act.wait_ge(s_ft, 4 * FRONT[part] + b + 1)
                A.go(act.activation(XTh[:, :, S * b:S * b + S],
                                    PS[bank][:, :].rearrange("p (k s) -> p k s", k=KD), ACT.Copy), s_xh)

            def router0():
                act.wait_ge(s_rp, 1)
                r = PS[7][:, 0:NT * 2 * E0].rearrange("p (t e) -> p t e", t=NT)
                A.go(act.activation(R(0), r[:, :, E0:2 * E0], ACT.Exp, scale=-1.0), s_ra)
                act.wait_ge(s_rv, 1)
                A.go(act.activation(R(1), R(1), ACT.Exp), s_ra)

            def copy_combine(layer, rows):
                act.wait_ge(s_cw, layer + 1)
                A.go(act.activation(combT[0:rows, :], PS[7][0:rows, :].bitcast(bf16), ACT.Copy), s_cT)

            def ffn(layer, nj):
                base, units = layer * 2 * NJ0, 2 * nj
                for n in range(units + 2):
                    if n < units:
                        act.wait_ge(s_gu, base + n + 1)
                        if n >= 2:
                            act.wait_ge(s_t1, base + n - 1)
                        A.go(act.activation(SI[:, n % 2, :], PS[2 + 2 * (n % 2)][:, :], ACT.Silu), s_si)
                    if n == 1:
                        copy_combine(layer, K0 if layer == 0 else K3)
                    if 1 <= n <= units:
                        m = n - 1
                        act.wait_ge(s_t2, base + m + 1)
                        if m >= 2:
                            act.wait_ge(s_dn, base + m - 1)
                        A.go(act.activation(Hh[:, m % 2, :], T2[:, 0:512], ACT.Copy), s_hh)

            for b in range(B):
                front_hi(1, b, 2 * b)
            router0()
            ffn(0, NJ0)

            def l1_qk_hi(b):
                act.wait_ge(s_qk, b + 1)
                for q in range(2):
                    A.go(act.activation(QK1h[:, b, q, :], PS[2 * b][:, q * S:q * S + S], ACT.Identity,
                                        bias=b1[:, q:q + 1]), s_qh if q else None)

            def l1_exp(b):
                act.wait_ge(s_mx, b + 1)
                for i in range(2):
                    A.go(act.activation(EX1[:, b, i, :], PS[2 * b + 1][:, i * S:i * S + S], ACT.Exp,
                                        bias=v1[:, 8 + 2 * b + i:9 + 2 * b + i],
                                        accum_out=v1[:, 16 + 2 * b + i:17 + 2 * b + i]), s_ex if i else None)

            def l1_attention_hi(b):
                act.wait_ge(s_tt, b + 1)
                A.go(act.activation(AT1h[:, b, :, :], PS[2 * b][:, :].rearrange("p (k s) -> p k s", k=2),
                                    ACT.Copy), s_ah)

            def l1_copy_x(b):
                act.wait_ge(s_qT, b + 1)
                A.go(act.activation(XQT1[:, b, :, :], PS[2 * b][:, 0:256].bitcast(bf16)
                                    .rearrange("p (k s) -> p k s", k=KD), ACT.Copy), s_q9)

            def l1_relu(b):
                act.wait_ge(s_up, b + 1)
                act.wait_ge(s_v8, 1)
                for i in range(2):
                    m = A.go(act.activation(HR1[:, b, i, :], PS[2 * b + i][:, :], ACT.Relu,
                                            scale=v1[:, 32 + 2 * b + i:33 + 2 * b + i]),
                             s_re if i and b % 2 == 0 else None)
                if b % 2:
                    act.wait_ge(s_act, m)
                    A.go(act.activation(HR1[:, b, :, :], HR1[:, b, :, :], ACT.Square), s_re)

            def l1_scale_h(b):
                act.wait_ge(s_v8, 2)
                for i in range(2):
                    A.go(act.activation(HR1[:, b, i, :], HR1[:, b, i, :], ACT.Identity, bias=magic[:, 0:1],
                                        scale=v1[:, 56 + 2 * b + i:57 + 2 * b + i]), s_hs if i else None)

            def l1_copy_h(b):
                act.wait_ge(s_hT, b + 1)
                A.go(act.activation(HT1[:, b, :, :], PS[2 * b][:, :].bitcast(bf16)
                                    .rearrange("p (c s) -> p c s", c=4), ACT.Copy), s_h9)

            act.wait_ge(s_in["rt"], 48)
            for step in (l1_qk_hi, l1_exp, l1_attention_hi, lambda b: front_hi(2, b, 2 * b)):
                for b in range(B):
                    step(b)
            for step in (l1_copy_x, l1_relu, l1_scale_h, l1_copy_h):
                for b in range(B):
                    step(b)

            def l2_square(n):
                act.wait_ge(s_hc, n + 1)
                g = n % 2
                A.go(act.activation(TM4[:, 4 * g:4 * g + 4, :, :].rearrange("p a h r -> p a (h r)"),
                                    KF[:, 2 * g:2 * g + 2, :, :].rearrange("p b a n -> p (b a) n"),
                                    ACT.Square), s_hq)

            def l2_heads_hi(n):
                act.wait_ge(s_hn, n + 1)
                if n >= 2:
                    act.wait_ge(s_k4, 2 * (n % 2) + 2)
                g = n % 2
                for at in (0, (16, 32)[n // 2]):
                    A.go(act.activation(HS2[:, 2 * g:2 * g + 2, :, :, at:at + 16]
                                        .rearrange("p b a h r -> p (b a) h r"),
                                        KF[:, 2 * g:2 * g + 2, :, :].rearrange("p b a (h r) -> p (b a) h r", h=H2),
                                        ACT.Copy), s_hp)

            def l2_values_hi():
                act.wait_ge(s_vf, 2 * B)
                act.wait_ge(s_in["l2"], 16 * 14)
                act.wait_ge(s_z2, 11)
                for kt in range(2):
                    vf = VF[:, kt, :, :].rearrange("p b (h r) -> p (b h) r", h=H2)
                    for part in range(kt + 1):
                        c = 17 * part
                        A.go(act.activation(VEh[:, kt, :, :, c:c + 16].rearrange("p b h r -> p (b h) r"), vf,
                                            ACT.Copy, scale=mask[:, kt, part:part + 1]), s_vh)

            def l2_copy_heads(n, dst):
                banks = (2 * (n % B), 2 * (n % B) + 1)
                act.wait_ge(s_k4, n + 1)
                for q in range(2):
                    A.go(act.activation(dst[:, 4 * q:4 * q + 4, :], PS[banks[q]][:, :].bitcast(f16)
                                        .rearrange("p (a s) -> p a s", a=4), ACT.Copy), s_k5)

            def l2_copy_maxima(b):
                act.wait_ge(s_mt, b + 1)
                for q in range(2):
                    A.go(act.activation(QT3[:, b, 4 * q:4 * q + 4, :], PS[6 + q][:, :].bitcast(f16)
                                        .rearrange("p (a s) -> p a s", a=4), ACT.Copy), s_mc if q else None)

            def l2_exp(g):
                act.wait_ge(s_st, g // 2 + 1)
                if g >= 4:
                    act.wait_ge(s_el, g - 3)
                A.go(act.activation(EX2[:, g % 4, :], PS[2 + g % 2][:, :], ACT.Exp, scale=HD2 ** -0.5), s_e2)

            def l2_copy_mixed(n):
                b, q = n // 4, n % 4
                act.wait_ge(s_pv, 4 * (n + 1))
                if q == 0 and b >= 1:
                    act.wait_ge(s_cx, b)
                A.go(act.activation(OB2[:, :, 4 * q:4 * q + 4, :], PS[4 + n % 2][:, 0:8 * VE]
                                    .rearrange("p (i h v) -> p i h v", i=2, h=4), ACT.Copy), s_ob)

            def l2_joined_hi(b):
                act.wait_ge(s_ct, b + 1)
                if b >= 1:
                    act.wait_ge(s_wo, b)
                A.go(act.activation(CXh, PS[7][:, :].rearrange("p (k s) -> p k s", k=KD), ACT.Copy), s_ch)

            def fp8_copy(b):
                act.wait_ge(s_t5, b + 1)
                A.go(act.activation(QT5[:, b, :, :], PS[2 * b][:, 0:256].bitcast(bf16)
                                    .rearrange("p (k s) -> p k s", k=KD), ACT.Copy), s_c5)

            for g in range(2):
                l2_square(g)
            l2_values_hi()
            for g in range(2):
                l2_heads_hi(g)
            for b in range(B):
                l2_copy_heads(b, KT3[:, b, :, :])
            for b in range(B):
                front_hi(4, b, 2 * b)
            for step in (l2_square, l2_heads_hi):
                for g in range(2):
                    step(2 + g)
            for b in range(B):
                l2_copy_heads(B + b, QT3[:, b, :, :])
            l2_copy_maxima(0)
            for k in range(B * NP2 + 4):
                b, p = k // NP2, k % NP2
                if b < B:
                    l2_exp(2 * k)
                    l2_exp(2 * k + 1)
                if p == TURN and b + 1 < B:
                    l2_copy_maxima(b + 1)
                if 2 <= k <= B * NP2 and k % 2 == 0:
                    l2_copy_mixed(k // 2 - 1)
                if b >= 1 and p == 3:
                    l2_joined_hi(b - 1)
            def l3_vo_hi(n):
                act.wait_ge(s_wv, n + 1)
                A.go(act.activation(WVh[:, 2 * n:2 * n + 2, :], PS[n][:, :].rearrange("p (h d) -> p h d", h=2),
                                    ACT.Copy), s_wh)

            def l3_weights_hi(n):
                act.wait_ge(s_ring[n % RING], 16 * (n // RING + 1))
                _, w, hi, _ = LOADS[n]
                A.go(act.activation(hi, ring[:, n % RING, 0:w], ACT.Copy), s_hi)

            def l3_taken(G, q, hi, sq, made, kq):
                act.wait_ge(made, 2 * G + q + 1)
                src = PS[1 + q][:, :]
                if G >= 1:
                    act.wait_ge(s_ss, 2 * G - 1 + kq)
                if G >= 2:
                    act.wait_ge(s_s3, HG * (G - 1))
                v = (KG3h, QG3h)[kq][:, G % 2, 2 * q:2 * q + 2, :]
                src3 = src.rearrange("p (h s) -> p h s", h=2)
                if kq == 0:
                    A.go(act.activation(v, src3, ACT.Copy, scale=g3[:, 2:3]), hi)
                else:
                    A.go(act.activation(v, src3, ACT.Copy), hi)
                A.go(act.activation(SQ3[:, kq, q, :], src, ACT.Square), sq)

            def l3_copy_parts(G):
                act.wait_ge(s_kt, G + 1)
                if G >= 1:
                    act.wait_ge(s_rb, 2 * G)
                A.go(act.activation(KR3[:, :], PS[7][0:3 * HG, 64:192].bitcast(bf16), ACT.Copy), s_kc)

            def l3_copy_rms(G, q):
                act.wait_ge(s_rb, 2 * G + q + 1)
                if G >= 2:
                    act.wait_ge(s_m3, 2 * HG * (G - 1))
                A.go(act.activation(RB3[:, G % 2, 2 * q:2 * q + 2, :], PS[7][:, :]
                                    .rearrange("p (h s) -> p h s", h=2), ACT.Copy), s_rc)

            def l3_make(G, j):
                if j == 0:
                    l3_taken(G, 0, s_kh, s_k2, s_kp, 0)
                    l3_taken(G, 1, s_kh, s_k2, s_kp, 0)
                elif j == 1:
                    l3_taken(G, 0, s_q3h, s_q32, s_q3, 1)
                    l3_taken(G, 1, s_q3h, s_q32, s_q3, 1)

            def l3_exp(n):
                G, h = n // HG, n % HG
                act.wait_ge(s_b3, n + 1)
                for i in range(2):
                    A.go(act.activation(SP3[:, n % 2, i, :], SP3[:, n % 2, i, :], ACT.Exp,
                                        bias=a3[:, n % 2, 2 + i:3 + i], scale=rs3[:, G % 2, 1, i, h:h + 1],
                                        accum_out=a3[:, n % 2, 4 + i:5 + i]), s_e3)

            def l3_turned_hi(n):
                act.wait_ge(s_t3, n + 1)
                if n >= 2:
                    act.wait_ge(s_c3, n - 1)
                A.go(act.activation(PT3h[:, n % 2, :, :], PS[5][:, :].rearrange("p (k s) -> p k s", k=2),
                                    ACT.Copy), s_th)

            def l3_mixed_hi(n):
                act.wait_ge(s_c3, n + 1)
                if n >= 2:
                    act.wait_ge(s_y3, n - 1)
                A.go(act.activation(OT3h[:, n % 2, :], PS[6][:, 0:S], ACT.Copy), s_oh)

            def router3():
                act.wait_ge(s_rp, 2)
                act.wait_ge(s_rv, 2)
                A.go(act.activation(rt8(0), PS[7][:, 0:NT * E3].rearrange("p (t e) -> p t e", t=NT), ACT.Exp,
                                    scale=tmp3[:, 1:2]), s_ra)
                act.wait_ge(s_rv, 3)
                A.go(act.activation(rt8(2), rt8(1), ACT.Exp, scale=-1.0 / 0.1), s_ra)
                A.go(act.activation(rt8(3), rt8(1), ACT.Exp, scale=-1.0 / 0.3), s_ra)

            for n in range(H3 // 2):
                l3_vo_hi(n)
            for n in range(QKW, QKW + 4):
                l3_weights_hi(n)
            for b in range(B):
                fp8_copy(b)
            for n in range(QKW + 4, FF3):
                l3_weights_hi(n)
            for b in range(B):
                front_hi(6, b, 2 * b)
            act.wait_ge(s_g3, 1)
            for j in range(2):
                l3_make(0, j)
            l3_copy_parts(0)
            for q in range(2):
                l3_copy_rms(0, q)
            N3 = B * H3
            for n in range(N3 + 4):
                spread = n % HG == HG - 1 and n < N3 - 1
                if n >= 4:
                    l3_mixed_hi(n - 4)
                if 2 <= n < N3 + 2:
                    l3_turned_hi(n - 2)
                if spread:
                    l3_copy_parts(n // HG + 1)
                if n // HG + 1 < NG:
                    l3_make(n // HG + 1, n % HG)
                if spread:
                    l3_copy_rms(n // HG + 1, 0)
                if n < N3:
                    l3_exp(n)
                if spread:
                    l3_copy_rms(n // HG + 1, 1)
            for b in range(B):
                front_hi(7, b, 2 * b)
            router3()
            ffn(1, NJ3)

        @block.vector
        def _(dve):
            V = Order(dve, s_dve)

            def rsqrt(v, n, y=None):
                y, g = nw[:, 1, 0:n], nw[:, 2, 0:n]
                V.do(dve.tensor_scalar(y.bitcast(i32), v.bitcast(i32), 1, None, ALU.logical_shift_right))
                V.do(dve.tensor_scalar(y.bitcast(i32), y.bitcast(i32), -1.0, float(0x5F3759DF),
                                       ALU.mult, ALU.add))
                for _ in range(3):
                    V.do(dve.tensor_tensor(g, y, y, ALU.mult))
                    V.do(dve.scalar_tensor_tensor(out=g, in0=g, scalar=-0.5, in1=v, op0=ALU.mult, op1=ALU.mult))
                    V.do(dve.scalar_tensor_tensor(out=y, in0=g, scalar=1.5, in1=y, op0=ALU.add, op1=ALU.mult))
                return y

            def layer_norm(part):
                for t in range(NT):
                    if part >= 1 and t % 2 == 0:
                        dve.wait_ge(s_x[part - 1], t // 2 + 1)
                    m = V.go(dve.bn_stats(st[:, t, :], X[:, t, :]))
                dve.wait_ge(s_dve, m)
                for t in range(NT):
                    m = V.go(dve.bn_aggr(mv[:, t, :], st[:, t, :]))
                dve.wait_ge(s_dve, m)
                v = nw[:, 0, 0:NT]
                V.do(dve.tensor_scalar(v, mv[:, :, 1], LN_EPS, None, ALU.add))
                y = rsqrt(v, NT)
                for t in range(NT):
                    V.go(dve.tensor_scalar(XN[:, t, :], X[:, t, :], mv[:, t, 0:1], y[:, t:t + 1],
                                           ALU.subtract, ALU.mult), s_ln if t % 2 else None)

            EPS = 1e-6

            def sq_factors(n):
                kc = 2 - n
                ax, rw, s, si = (sq[:, :, q:q + kc] for q in (0, 2 + 2 * n, 24, 8))
                r = nw[:, 3, 0:B * kc].rearrange("p (b k) -> p b k", b=B)
                for b in range(B):
                    dve.wait_ge(s_xt, 4 * n + b + 1)
                    m = V.go(dve.tensor_reduce(sq[:, b, 0:kc], PS[2 * b][:, 0:kc * S]
                                               .rearrange("p (k s) -> p k s", k=kc),
                                               AX.X, ALU.max, apply_absolute_value=True))
                dve.wait_ge(s_dve, m)
                V.do(dve.scalar_tensor_tensor(out=r, in0=ax, scalar=EPS, in1=rw, op0=ALU.max, op1=ALU.mult))
                y = rsqrt(nw[:, 3, 0:B * kc], B * kc).rearrange("p (b k) -> p b k", b=B)
                V.do(dve.tensor_tensor(s, r, y, ALU.mult))
                V.do(dve.tensor_scalar(s, s, EPS, None, ALU.max))
                V.do(dve.reciprocal(si, s), s_iv)
                for b in range(B):
                    for k in range(kc):
                        w = guT[:, b, k, :] if n == 0 else ctT[:, b, :]
                        V.go(dve.tensor_scalar(QS[:, b, 2 + k, :], w, sq[:, b, 24 + k:25 + k], None, ALU.mult),
                             s_ws if k == kc - 1 else None)

            def sq_steps(n):
                w = 128 * (2 - n)
                am, sc, iv = (sq[:, :, q:q + 4] for q in (12, 20, 16))
                for b in range(B):
                    dve.wait_ge(s_bk, 4 * n + b + 1)
                    for j in range(2):
                        m = V.go(dve.tensor_reduce(sq[:, b, 12 + 2 * j:14 + 2 * j],
                                                   PS[2 * b + j][:, 0:2 * w].rearrange("p (i w) -> p i w", i=2),
                                                   AX.X, ALU.max, apply_absolute_value=True))
                dve.wait_ge(s_dve, m)
                V.do(dve.tensor_scalar(sc, am, EPS, 1.0 / 127.0, ALU.max, ALU.mult))
                V.do(dve.reciprocal(iv, sc), s_iv)
                for b in range(B):
                    for i in range(2):
                        V.go(dve.tensor_scalar(DG[:, b, i, :], idf[:, :], sq[:, b, 22 + i:23 + i], None,
                                               ALU.mult), s_dg if i else None)

            def sq_clip(n, b):
                w = 128 * (2 - n)
                dve.wait_ge(s_rd, 4 * n + b + 1)
                q = QS[:, b, :, 0:w]
                V.do(dve.tensor_scalar(q, q, MAGIC, 127.0, ALU.subtract, ALU.min))
                V.go(dve.tensor_scalar(QB[:, b, :, 0:w], q, -127.0, None, ALU.max), s_qb)

            def sq_out(n, b):
                dve.wait_ge(s_wb, 4 * n + b + 1)
                for i in range(2):
                    m = V.go(dve.scalar_tensor_tensor(out=HU[:, b, i, :], in0=PS[2 * b + 1][:, i * S:i * S + S],
                                                      scalar=sq[:, b, 20 + i:21 + i], in1=WB[:, b, :],
                                                      op0=ALU.mult, op1=ALU.mult),
                             s_hu if n == 0 and i else None)
                if n == 1:
                    dve.wait_ge(s_dve, m)
                    V.go(dve.tensor_tensor(X[:, 2 * b:2 * b + 2, :], X[:, 2 * b:2 * b + 2, :],
                                           HU[:, b, :, :], ALU.add), s_x[0])

            dve.wait_ge(s_in["x"], 16)
            layer_norm(0)
            dve.wait_ge(s_in["gu"], 16)
            dve.wait_ge(s_in["ct"], 16)
            V.go(dve.tensor_reduce(sq[:, :, 2:4], guT, AX.X, ALU.max, apply_absolute_value=True))
            V.do(dve.tensor_reduce(sq[:, :, 4], ctT, AX.X, ALU.max, apply_absolute_value=True))
            V.do(dve.tensor_scalar(sq[:, :, 2:5], sq[:, :, 2:5], EPS, None, ALU.max))
            V.do(dve.reciprocal(sq[:, :, 2:5], sq[:, :, 2:5]))
            for n in range(2):
                sq_factors(n)
                sq_steps(n)
                for step in (sq_clip, sq_out):
                    for b in range(B):
                        step(n, b)
                if n == 0:
                    for b in range(B):
                        dve.wait_ge(s_sl, b + 1)
                        V.go(dve.tensor_tensor(HA[:, b, :, :], HA[:, b, :, :], HU[:, b, :, 128:256],
                                               ALU.mult), s_ha)

            def front_lo(part, b, bank):
                dve.wait_ge(s_ft, 4 * FRONT[part] + b + 1)
                dve.wait_ge(s_xh, 4 * FRONT[part] + b + 1)
                V.go(dve.tensor_tensor(XTl[:, :, S * b:S * b + S],
                                       PS[bank][:, :].rearrange("p (k s) -> p k s", k=KD),
                                       XTh[:, :, S * b:S * b + S], ALU.subtract), s_xl)

            def over(v, e):
                return v.unsqueeze(2).broadcast_to([128, NT, e])

            def top2(val, e, mask, tmp):
                for t in range(NT):
                    m = V.go(dve.max(top8[:, t, :], val[:, t, :]))
                dve.wait_ge(s_dve, m)
                for t in range(NT):
                    m = V.go(dve.max_index(idx8[:, t, :], top8[:, t, :], val[:, t, :]))
                dve.wait_ge(s_dve, m)
                V.do(dve.tensor_copy(idxf, idx8))
                it = iota_b[:, 0:e].unsqueeze(1).broadcast_to([128, NT, e])
                V.go(dve.tensor_tensor(mask, it, over(idxf[:, :, 0], e), ALU.is_equal))
                V.do(dve.tensor_tensor(tmp, it, over(idxf[:, :, 1], e), ALU.is_equal))
                V.do(dve.tensor_tensor(mask, mask, tmp, ALU.add))

            def split3(w, e, ones):
                st_ = E0 + 1 if ones else e
                t = R(4)[:, :, 0:e]
                V.do(dve.tensor_copy(CM[:, :, 0:e], w))
                V.do(dve.tensor_tensor(t, w, CM[:, :, 0:e], ALU.subtract))
                V.do(dve.tensor_copy(CM[:, :, st_:st_ + e], t))
                V.do(dve.tensor_tensor(CM[:, :, 2 * st_:2 * st_ + e], t, CM[:, :, st_:st_ + e], ALU.subtract), s_cm)

            def router0():
                r = PS[7][:, 0:NT * 2 * E0].rearrange("p (t e) -> p t e", t=NT)
                lg, ab, e1, sc, mx = R(2), R(1), R(0), R(3), rt[:, 5, 0:NT]
                dve.wait_ge(s_in["rt"], 48)
                dve.wait_ge(s_ra, 1)
                V.do(dve.tensor_scalar(e1, e1, 1.0, None, ALU.add))
                V.do(dve.reciprocal(e1, e1))
                V.do(dve.tensor_tensor(e1, r[:, :, E0:2 * E0], e1, ALU.mult))
                V.do(dve.tensor_tensor(lg, r[:, :, 0:E0], e1, ALU.mult))
                V.do(dve.scalar_tensor_tensor(out=ab, in0=lg, scalar=-1.0, in1=lg, op0=ALU.mult, op1=ALU.max))
                V.do(dve.tensor_reduce(mx, ab, AX.X, ALU.max))
                V.go(dve.tensor_tensor(ab, ab, over(mx, E0), ALU.subtract), s_rv)
                dve.wait_ge(s_ra, 2)
                V.do(dve.tensor_reduce(mx, ab, AX.X, ALU.add))
                V.do(dve.reciprocal(mx, mx))
                V.do(dve.tensor_tensor(sc, ab, over(mx, E0), ALU.mult))
                V.do(dve.tensor_tensor(lg, sc, rta[:, 1, :].unsqueeze(1).broadcast_to([128, NT, E0]), ALU.add))
                top2(lg, E0, e1, ab)
                V.do(dve.tensor_tensor(sc, sc, rta[:, 0, :].unsqueeze(1).broadcast_to([128, NT, E0]), ALU.mult))
                V.do(dve.scalar_tensor_tensor(out=sc, in0=sc, scalar=1.0, in1=e1, op0=ALU.add, op1=ALU.mult))
                V.do(dve.memset(CM[:, :, :], 0.0))
                V.do(dve.memset(CM[:, :, E0:E0 + 1], 1.0))
                split3(sc, E0, True)

            def ternary(part):
                if part == 0:
                    dve.wait_ge(s_in["tw"], 32)
                    V.go(dve.tensor_reduce(v1[:, 0:1], rawU, AX.X, ALU.add, apply_absolute_value=True))
                    V.go(dve.tensor_reduce(v1[:, 1:2], rawD, AX.X, ALU.add, apply_absolute_value=True), s_pa)
                    return
                if part == 1:
                    dve.wait_ge(s_ps, 1)
                    V.do(dve.tensor_scalar(v1[:, 2:4], PS[7][:, 0:2], 1.0 / (512 * D), 1e-5, ALU.mult, ALU.max))
                    V.do(dve.reciprocal(v1[:, 4:6], v1[:, 2:4]))
                raw, w, q = ((rawU, TWu), (rawD, TWd))[part - 1] + (part - 1,)
                V.do(dve.tensor_scalar(raw, raw, v1[:, 4 + q:5 + q], MAGIC, ALU.mult, ALU.add))
                V.do(dve.tensor_scalar(raw, raw, MAGIC, 1.0, ALU.subtract, ALU.min))
                V.go(dve.tensor_scalar(w.rearrange("p a b -> p (a b)"), raw, -1.0, None, ALU.max), s_tw)

            def centre_heads(w, n, sm=None):
                sums = nw[:, 3, 0:n]
                V.do(dve.tensor_reduce(sums, w, AX.X, ALU.add))
                V.go(dve.scalar_tensor_tensor(out=w, in0=sums.unsqueeze(2).broadcast_to([128, n, HD2]),
                                              scalar=-1.0 / HD2, in1=w, op0=ALU.mult, op1=ALU.add), sm)

            def centre_weights(q):
                n = L2W + q
                dve.wait_ge(s_ring[n % RING], 16 * (n // RING + 1))
                c = 2 * D if q == 0 else D
                if q:
                    dve.wait_ge(s_lc, q)
                centre_heads(ring[:, n % RING, 0:c].rearrange("p (h r) -> p h r", r=HD2), c // HD2, s_lc)

            def ffn(layer, nj):
                base, units = layer * 2 * NJ0, 2 * nj
                last = 1 if layer == 0 else 7
                for n in range(units + 2):
                    if n < units:
                        dve.wait_ge(s_si, base + n + 1)
                        V.go(dve.tensor_tensor(T1[:, n % 2, :], SI[:, n % 2, :], PS[3 + 2 * (n % 2)][:, :],
                                               ALU.mult), s_t1)
                    if 1 <= n <= units:
                        m = n - 1
                        dve.wait_ge(s_cb, base + m // SAME[layer] + 1)
                        dve.wait_ge(s_t1, base + m + 1)
                        if m >= 1:
                            dve.wait_ge(s_hl, base + m)
                        V.go(dve.tensor_tensor(T2[:, 0:512], T1[:, m % 2, :], PS[6][:, :], ALU.mult), s_t2)
                        dve.wait_ge(s_t2, base + m + 1)
                        dve.wait_ge(s_hh, base + m + 1)
                        V.go(dve.tensor_tensor(Hl[:, m % 2, :], T2[:, 0:512], Hh[:, m % 2, :],
                                               ALU.subtract), s_hl)
                    if layer == 0 and CENTRE <= n < CENTRE + 3:
                        centre_weights(n - CENTRE)
                    if layer == 0 and n in (TERNARY, TERNARY + 2, TERNARY + 4):
                        ternary((n - TERNARY) // 2)
                    if n in (nj + 1, units + 1):
                        h = n // nj - 1 if n == nj + 1 else 1
                        dve.wait_ge(s_dn, base + (h + 1) * nj)
                        for i in range(2):
                            t = 4 * h + 2 * i
                            V.go(dve.tensor_tensor(X[:, t:t + 2, :], X[:, t:t + 2, :],
                                                   PS[i][:, :].rearrange("p (t d) -> p t d", t=2), ALU.add),
                                 s_x[last])

            layer_norm(1)
            for b in range(B):
                front_lo(1, b, 2 * b)
            router0()
            ffn(0, NJ0)

            def l1_qk_lo(b):
                dve.wait_ge(s_qk, b + 1)
                dve.wait_ge(s_qh, b + 1)
                for q in range(2):
                    V.go(dve.scalar_tensor_tensor(out=QK1l[:, b, q, :], in0=PS[2 * b][:, q * S:q * S + S],
                                                  scalar=b1[:, q:q + 1], in1=QK1h[:, b, q, :],
                                                  op0=ALU.add, op1=ALU.subtract), s_ql if q else None)

            def l1_max(b):
                dve.wait_ge(s_en, b + 1)
                V.go(dve.tensor_reduce(v1[:, 8 + 2 * b:10 + 2 * b], PS[2 * b + 1][:, :]
                                       .rearrange("p (i s) -> p i s", i=2), AX.X, ALU.max, negate=True), s_mx)

            def l1_attention(b):
                dve.wait_ge(s_ex, b + 1)
                r = v1[:, 24 + 2 * b:26 + 2 * b]
                V.do(dve.reciprocal(r, v1[:, 16 + 2 * b:18 + 2 * b]))
                for i in range(2):
                    V.go(dve.tensor_scalar(EX1[:, b, i, :], EX1[:, b, i, :], r[:, i:i + 1], None, ALU.mult),
                         s_an if i else None)

            def l1_attention_lo(b):
                dve.wait_ge(s_tt, b + 1)
                dve.wait_ge(s_ah, b + 1)
                V.go(dve.tensor_tensor(AT1l[:, b, :, :], PS[2 * b][:, :].rearrange("p (k s) -> p k s", k=2),
                                       AT1h[:, b, :, :], ALU.subtract), s_at)

            def l1_add(b):
                dve.wait_ge(s_xm, b + 1)
                V.go(dve.tensor_tensor(X[:, 2 * b:2 * b + 2, :], X[:, 2 * b:2 * b + 2, :],
                                       PS[2 * b + 1][:, :].rearrange("p (t d) -> p t d", t=2), ALU.add), s_x[2])

            def steps8(am, sc, iv, to):
                V.do(dve.tensor_scalar(sc, am, 1e-5, 1.0 / 127.0, ALU.max, ALU.mult))
                V.do(dve.reciprocal(iv, sc))
                V.do(dve.tensor_scalar(sc, sc, v1[:, to:to + 1], None, ALU.mult), s_v8)

            def l1_quant_x():
                for b in range(B):
                    dve.wait_ge(s_ln, 4 * 3 + b + 1)
                    m = V.go(dve.tensor_reduce(v1[:, 40 + 2 * b:42 + 2 * b], XN[:, 2 * b:2 * b + 2, :], AX.X,
                                               ALU.max, apply_absolute_value=True))
                dve.wait_ge(s_dve, m)
                steps8(v1[:, 40:48], v1[:, 32:40], v1[:, 56:64], 2)
                for b in range(B):
                    for i in range(2):
                        m = V.go(dve.tensor_scalar(XF1[:, b, i, :], XN[:, 2 * b + i, :],
                                                   v1[:, 56 + 2 * b + i:57 + 2 * b + i], MAGIC, ALU.mult, ALU.add))
                    dve.wait_ge(s_dve, m)
                    V.do(dve.tensor_scalar(XF1[:, b, :, :], XF1[:, b, :, :], MAGIC, 127.0, ALU.subtract, ALU.min))
                    V.go(dve.tensor_scalar(XQ1[:, b, :, :], XF1[:, b, :, :], -127.0, None, ALU.max), s_q8)

            def l1_quant_h():
                for b in range(B):
                    dve.wait_ge(s_re, b + 1)
                    if b % 2 == 0:
                        m = V.go(dve.tensor_tensor(HR1[:, b, :, :], HR1[:, b, :, :], HR1[:, b, :, :], ALU.mult))
                    if b >= 1:
                        V.go(dve.tensor_reduce(v1[:, 38 + 2 * b:40 + 2 * b], HR1[:, b - 1, :, :], AX.X, ALU.max,
                                               apply_absolute_value=True))
                    dve.wait_ge(s_dve, m)
                m = V.go(dve.tensor_reduce(v1[:, 46:48], HR1[:, B - 1, :, :], AX.X, ALU.max,
                                           apply_absolute_value=True))
                dve.wait_ge(s_dve, m)
                steps8(v1[:, 40:48], v1[:, 48:56], v1[:, 56:64], 3)
                for b in range(B):
                    dve.wait_ge(s_hs, b + 1)
                    V.go(dve.tensor_scalar(HQ1[:, b, :, :], HR1[:, b, :, :], MAGIC, 127.0, ALU.subtract, ALU.min),
                         s_h8)

            def l1_out(b):
                dve.wait_ge(s_d1, b + 1)
                for i in range(2):
                    t = 2 * b + i
                    V.go(dve.scalar_tensor_tensor(out=X[:, t, :], in0=PS[2 * b + 1][:, i * D:i * D + D],
                                                  scalar=v1[:, 48 + t:49 + t], in1=X[:, t, :],
                                                  op0=ALU.mult, op1=ALU.add), s_x[3] if i else None)

            dve.wait_ge(s_in["rt"], 48)
            layer_norm(2)
            for step in (l1_qk_lo, l1_max, l1_attention, l1_attention_lo, lambda b: front_lo(2, b, 2 * b),
                         l1_add):
                for b in range(B):
                    step(b)
            layer_norm(3)
            l1_quant_x()
            l1_quant_h()
            for b in range(B):
                l1_out(b)

            def bc(v, shape, *axes):
                for a in axes:
                    v = v.unsqueeze(a)
                return v.broadcast_to(shape)

            def l2_heads(kq, lo):
                n, v = NT * H2, KF.rearrange("p b a (h r) -> p (b a) h r", h=H2)
                sqs = nw[:, 4, 0:n].rearrange("p (a h) -> p a h", a=NT)
                halves = (slice(0, 4), slice(4, 8))
                part = [4, H2, HD2]
                full = [128] + part

                def col(w, a):
                    return w[:, a, :].unsqueeze(3).broadcast_to(full)

                for g, a in enumerate(halves):
                    dve.wait_ge(s_hq, 2 * kq + g + 1)
                    m = V.go(dve.tensor_reduce(sqs[:, a, :], TM4[:, a, :, :], AX.X, ALU.add))
                dve.wait_ge(s_dve, m)
                q = nw[:, 4, 0:n]
                V.do(dve.tensor_scalar(q, q, 1.0 / HD2, 1e-6, ALU.mult, ALU.add))
                y = rsqrt(q, n).rearrange("p (a h) -> p a h", a=NT)
                dve.wait_ge(s_hc, 2 * kq + 2)
                for a in halves:
                    m = V.go(dve.tensor_tensor(v[:, a, :, :], v[:, a, :, :], col(y, a), ALU.mult))
                dve.wait_ge(s_dve, m)
                for w, op in enumerate((ALU.mult, ALU.add)):
                    for g in range(2):
                        for kt in range(2):
                            a = slice(4 * g + kt, 4 * g + kt + 3, 2)
                            aff = KG2[:, kt, w, :] if kq == 0 else QG2[:, w, :]
                            m = V.go(dve.tensor_tensor(v[:, a, :, :], v[:, a, :, :],
                                                       bc(aff, [128, 2, H2, HD2], 1, 1), op),
                                     s_hn if w and kt else None)
                    if w == 0:
                        dve.wait_ge(s_dve, m)
                dve.wait_ge(s_dve, m)
                for g in range(2):
                    dve.wait_ge(s_hn, 2 * kq + g + 1)
                    dve.wait_ge(s_hp, 4 * kq + 2 * g + 2)
                    for b in (2 * g, 2 * g + 1):
                        V.go(dve.tensor_tensor(HS2[:, b, :, :, lo:lo + 16], v[:, 2 * b:2 * b + 2, :, :],
                                               HS2[:, b, :, :, 0:16], ALU.subtract), s_k3 if b % 2 else None)

            def l2_keys():
                dve.wait_ge(s_in["l2"], 16 * 14)
                dve.wait_ge(s_z2, 5)
                dve.wait_ge(s_lc, 3)
                for a in range(2):
                    centre_heads(BKV[:, a, 0:D].rearrange("p (h r) -> p h r", r=HD2), H2, s_lc)
                    dve.wait_ge(s_lc, 4 + a)
                centre_heads(BQO[:, 0, :].rearrange("p (h r) -> p h r", r=HD2), H2, s_lc)
                dve.wait_ge(s_lc, 6)
                for b in range(B):
                    dve.wait_ge(s_kv, b + 1)
                    for kt in range(2):
                        for dst, c, w in ((VF[:, kt, b, :], D, s_vf), (KF[:, b, kt, :], 0, None)):
                            if b % 2 and kt and not w:
                                w = s_hc
                            V.go(dve.tensor_tensor(dst, PS[2 * b + kt][:, c:c + D], BKV[:, kt, c:c + D],
                                                   ALU.add), w)
                l2_heads(0, 32)

            def l2_values_lo():
                vf = VF[:, 1, :, :].rearrange("p b (h r) -> p (b h) r", h=H2)
                for part in range(2):
                    c, w = 17 * part, mask[:, 1, part:part + 1]
                    hi, lo = (v[:, 1, :, :, c:c + 16].rearrange("p b h r -> p (b h) r") for v in (VEh, VEl))
                    dve.wait_ge(s_vh, 2 + part)
                    V.go(dve.scalar_tensor_tensor(out=lo, in0=vf, scalar=w, in1=hi,
                                                  op0=ALU.mult, op1=ALU.subtract))

            def l2_queries():
                dve.wait_ge(s_k4, B)
                V.do(dve.memset(HS2[:, :, :, :, 48:50], 0.0))
                for b in range(B):
                    dve.wait_ge(s_qp, b + 1)
                    V.go(dve.tensor_tensor(KF[:, b, :, :], PS[2 * b + 1][:, :].rearrange("p (a n) -> p a n", a=2),
                                           bc(BQO[:, 0, :], [128, 2, D], 1), ALU.add), s_hc if b % 2 else None)
                l2_heads(1, 16)

            def l2_max(b, h):
                dve.wait_ge(s_s2, (H2 * b + h) // 2 + 1)
                s_ = PS[bank2(NP2 * b + h // 2) + h % 2][:, :].rearrange("p (i s) -> p i s", i=2)
                for q, keys in enumerate((slice(0, S - DCA), slice(S - DCA, S))):
                    V.go(dve.tensor_reduce(HS2[:, b, :, h, 48 + q], s_[:, :, keys], AX.X, ALU.max, negate=True),
                         s_m2)

            def l2_exp_hi(g):
                dve.wait_ge(s_e2, g + 1)
                if g >= 4:
                    dve.wait_ge(s_pv, g - 3)
                V.go(dve.tensor_copy(Eh2[:, g % 4, :], EX2[:, g % 4, :]), s_eh)

            def l2_join(b):
                dve.wait_ge(s_ob, 4 * (b + 1))
                if b >= 1:
                    dve.wait_ge(s_ct, b)
                rr = nw[:, 3:5, 0:2 * H2]
                o4 = OB2.rearrange("p i h (q v) -> p (i h) q v", q=2)
                V.do(dve.reciprocal(rr, o4[:, :, :, 16].rearrange("p n q -> p q n")))
                c3 = CX2.rearrange("p i (h r) -> p (i h) r", h=H2)
                shape = [128, 2 * H2, HD2]
                tm = TM2.rearrange("p (n r) -> p n r", r=HD2)
                V.go(dve.tensor_tensor(tm, o4[:, :, 0, 0:16], bc(rr[:, 0, :], shape, 2), ALU.mult))
                V.do(dve.tensor_tensor(c3, o4[:, :, 1, 0:16], bc(rr[:, 1, :], shape, 2), ALU.mult))
                V.go(dve.tensor_tensor(c3, c3, tm, ALU.add), s_cx)

            def l2_joined_lo(b):
                dve.wait_ge(s_ch, b + 1)
                V.go(dve.tensor_tensor(CXl, PS[7][:, :].rearrange("p (k s) -> p k s", k=KD), CXh,
                                       ALU.subtract), s_cl)

            def l2_add(b):
                dve.wait_ge(s_wo, b + 1)
                xb = X[:, 2 * b:2 * b + 2, :]
                V.do(dve.tensor_tensor(xb, xb, PS[6][:, :].rearrange("p (i n) -> p i n", i=2), ALU.add))
                V.go(dve.tensor_tensor(xb, xb, bc(BQO[:, 1, :], [128, 2, D], 1), ALU.add), s_x[4])

            def fp8_weights():
                dve.wait_ge(s_in["w8"], 48)
                V.do(dve.tensor_copy(v5[:, 1:2], v5b[:, 0:1]))
                V.do(dve.reciprocal(v5[:, 2:3], v5[:, 1:2]))
                V.do(dve.tensor_tensor(v5[:, 3:4], v5[:, 0:1], v5[:, 1:2], ALU.mult))
                V.do(dve.tensor_copy(w8i, w8r))
                V.go(dve.tensor_scalar(w8b, w8i, 128.0, -2.0, ALU.is_ge, ALU.mult))
                V.do(dve.tensor_scalar(w8a.bitcast(i32), w8i, 127, None, ALU.bitwise_and))
                V.go(dve.tensor_scalar(w8i, w8a.bitcast(i32), 20, None, ALU.logical_shift_left))
                V.do(dve.tensor_scalar(w8a, w8a.bitcast(i32), 2.0 ** -9, None, ALU.mult))
                V.do(dve.scalar_tensor_tensor(out=w8a, in0=w8i.bitcast(f32), scalar=2.0 ** 120, in1=w8a,
                                              op0=ALU.mult, op1=ALU.max))
                V.go(dve.scalar_tensor_tensor(out=W8[:, :], in0=w8b, scalar=1.0, in1=w8a,
                                              op0=ALU.add, op1=ALU.mult), s_w8)

            def fp8_quant():
                steps = (
                    lambda b, v, m: dve.tensor_scalar(v, XNr[:, 2 * D * b:2 * D * b + 2 * D], v5[:, 2:3], 448.0,
                                                      ALU.mult, ALU.min),
                    lambda b, v, m: dve.tensor_scalar(v, v, -448.0, None, ALU.max),
                    lambda b, v, m: dve.tensor_scalar(m.bitcast(i32), v.bitcast(i32), 0x7F800000, None,
                                                      ALU.bitwise_and),
                    lambda b, v, m: dve.tensor_scalar(m, m, 2.0 ** -6, 1.5 * 2.0 ** 20, ALU.max, ALU.mult),
                    lambda b, v, m: dve.tensor_tensor(v, v, m, ALU.add))
                dve.wait_ge(s_ln, 4 * 5 + B)
                done = [0] * B
                for step in steps:
                    for b in range(B):
                        if done[b]:
                            dve.wait_ge(s_dve, done[b])
                        done[b] = V.go(step(b, V5[:, b, :], M5[:, b, :]))
                for b in range(B):
                    dve.wait_ge(s_dve, done[b])
                    V.go(dve.tensor_tensor(Q5[:, b, :, :].rearrange("p i n -> p (i n)"), V5[:, b, :], M5[:, b, :],
                                           ALU.subtract), s_q5)

            def fp8_out(b):
                dve.wait_ge(s_p5, b + 1)
                for i in range(2):
                    t = 2 * b + i
                    V.go(dve.scalar_tensor_tensor(out=X[:, t, :], in0=PS[2 * b + 1][:, i * D:i * D + D],
                                                  scalar=v5[:, 3:4], in1=X[:, t, :],
                                                  op0=ALU.mult, op1=ALU.add), s_x[5] if i else None)

            l2_keys()
            layer_norm(4)
            l2_values_lo()
            for b in range(B):
                front_lo(4, b, 2 * b)
            l2_queries()
            for n in range(AHEAD):
                for h in (2 * (n % NP2), 2 * (n % NP2) + 1):
                    l2_max(n // NP2, h)
            for k in range(B * NP2 + 5):
                b, p = k // NP2, k % NP2
                for q in range(2):
                    if b < B:
                        l2_exp_hi(2 * k + q)
                for q in range(2):
                    if k + AHEAD < B * NP2:
                        l2_max((k + AHEAD) // NP2, 2 * ((k + AHEAD) % NP2) + q)
                if b >= 1 and p == 2:
                    l2_join(b - 1)
                if b >= 1 and p == 3:
                    l2_joined_lo(b - 1)
                if b >= 1 and p == 4:
                    l2_add(b - 1)

            def l3_vo_lo(n):
                dve.wait_ge(s_wv, n + 1)
                dve.wait_ge(s_wh, n + 1)
                V.go(dve.tensor_tensor(WVl[:, 2 * n:2 * n + 2, :], PS[n][:, :].rearrange("p (h d) -> p h d", h=2),
                                       WVh[:, 2 * n:2 * n + 2, :], ALU.subtract), s_wl)

            def lora(c):
                n = EARLY + c
                dve.wait_ge(s_lo, c + 1)
                dve.wait_ge(s_ring[n % RING], 16 * (n // RING + 1))
                r = ring[:, n % RING, :]
                V.go(dve.tensor_tensor(r[:, 0:512], r[:, 0:512], PS[2 * c][:, :], ALU.add))
                V.go(dve.tensor_tensor(r[:, 512:CH], r[:, 512:CH], PS[2 * c + 1][:, 0:D], ALU.add), s_la)

            def l3_lows(G, q, kq):
                made, hi, lo = ((s_kp, s_kh, s_kl), (s_q3, s_q3h, s_q3l))[kq]
                dve.wait_ge(made, 2 * G + q + 1)
                dve.wait_ge(hi, 2 * G + q + 1)
                dve.wait_ge((s_k2, s_q32)[kq], 2 * G + q + 1)
                if G >= 2:
                    dve.wait_ge(s_s3, HG * (G - 1))
                src = PS[1 + q][:, :].rearrange("p (h s) -> p h s", h=2)
                vh, vl = (v[:, G % 2, 2 * q:2 * q + 2, :] for v in ((KG3h, KG3l), (QG3h, QG3l))[kq])
                if kq == 0:
                    V.go(dve.scalar_tensor_tensor(out=vl, in0=src, scalar=g3[:, 2:3], in1=vh,
                                                  op0=ALU.mult, op1=ALU.subtract), lo)
                else:
                    V.go(dve.tensor_tensor(vl, src, vh, ALU.subtract), lo)

            def l3_sums(G, kq):
                dve.wait_ge(s_ss, 2 * G + kq + 1)
                if G >= 2:
                    dve.wait_ge(s_e3, 2 * HG * (G - 1))
                r = rs3[:, G % 2, kq, :, :].rearrange("p i h -> p (i h)")
                src = PS[7][:, 2 * HG * kq:2 * HG * (kq + 1)]
                if kq == 0:
                    V.go(dve.tensor_scalar(r, src, 1.0 / HD3, 1e-5, ALU.mult, ALU.add), s_sv)
                else:
                    V.go(dve.tensor_scalar(r, src, HD3 * 1e-5, None, ALU.add), s_sv)

            def l3_make(G, j):
                if j == 0:
                    l3_lows(G, 0, 0)
                    l3_lows(G, 1, 0)
                elif j == 1:
                    l3_lows(G, 0, 1)
                    l3_lows(G, 1, 1)

            def l3_scale(n):
                G, h, a = n // HG, n % HG, a3[:, n % 2, :]
                dve.wait_ge(s_s3, n + 1)
                dve.wait_ge(s_rc, 2 * G + h // 2 + 1)
                dve.wait_ge(s_rs, G + 1)
                if n >= 2:
                    dve.wait_ge(s_t3, n - 1)
                for i in range(2):
                    V.go(dve.tensor_tensor_reduce(SP3[:, n % 2, i, :], PS[3 + n % 2][:, i * S:i * S + S],
                                                  RB3[:, G % 2, h, :], 1.0, -3.0e38, ALU.mult, ALU.max,
                                                  a[:, i:i + 1]), s_m3)
                dve.wait_ge(s_m3, 2 * (n + 1))
                V.go(dve.scalar_tensor_tensor(out=a[:, 2:4], in0=a[:, 0:2], scalar=-1.0,
                                              in1=rs3[:, G % 2, 1, :, h], op0=ALU.mult, op1=ALU.mult), s_b3)

            def l3_normal(n):
                a = a3[:, n % 2, :]
                dve.wait_ge(s_e3, 2 * (n + 1))
                V.do(dve.reciprocal(a[:, 6:8], a[:, 4:6]))
                for i in range(2):
                    V.go(dve.tensor_scalar(SP3[:, n % 2, i, :], SP3[:, n % 2, i, :], a[:, 6 + i:7 + i], None,
                                           ALU.mult), s_n3 if i else None)

            def l3_turned_lo(n):
                dve.wait_ge(s_th, n + 1)
                V.go(dve.tensor_tensor(PT3l[:, n % 2, :, :], PS[5][:, :].rearrange("p (k s) -> p k s", k=2),
                                       PT3h[:, n % 2, :, :], ALU.subtract), s_tl)

            def l3_mixed_lo(n):
                dve.wait_ge(s_oh, n + 1)
                V.go(dve.tensor_tensor(OT3l[:, n % 2, :], PS[6][:, 0:S], OT3h[:, n % 2, :], ALU.subtract), s_ol)

            def l3_add(b):
                dve.wait_ge(s_y3, H3 * (b + 1))
                xb = X[:, 2 * b:2 * b + 2, :]
                V.go(dve.tensor_tensor(xb, xb, PS[0][:, :].rearrange("p (i n) -> p i n", i=2), ALU.add), s_x[6])

            def router3():
                centre, low, high = 0.36787944117144233, 0.5 - 0.28768207245178085, 0.5
                dve.wait_ge(s_in["g3"], 32)
                V.do(dve.reciprocal(tmp3[:, 1:2], tmp3[:, 0:1]))
                V.go(dve.tensor_scalar(tmp3[:, 1:2], tmp3[:, 1:2], -1.0, None, ALU.mult), s_rv)
                dve.wait_ge(s_ra, 3)
                e, d, w, fb, zone, t = (rt8(i) for i in range(6))
                mx, mn = rt[:, 6, 0:NT], rt[:, 7, 0:NT]
                V.do(dve.tensor_scalar(e, e, 1.0, None, ALU.add))
                V.do(dve.reciprocal(e, e))
                V.do(dve.tensor_scalar(zone, e, low, None, ALU.is_ge))
                V.do(dve.scalar_tensor_tensor(out=zone, in0=e, scalar=high, in1=zone, op0=ALU.is_le, op1=ALU.mult))
                V.do(dve.tensor_scalar(t, e, centre, None, ALU.subtract))
                V.go(dve.scalar_tensor_tensor(out=d, in0=t, scalar=-1.0, in1=t, op0=ALU.mult, op1=ALU.max), s_rv)
                dve.wait_ge(s_ra, 5)
                V.do(dve.tensor_tensor(w, w, zone, ALU.mult))
                top2(fb, E3, zone, t)
                V.do(dve.tensor_tensor(fb, fb, zone, ALU.mult))
                V.do(dve.tensor_reduce(mx, fb, AX.X, ALU.add))
                V.do(dve.tensor_scalar(mx, mx, 1e-8, None, ALU.max))
                V.do(dve.reciprocal(mx, mx))
                V.do(dve.tensor_tensor(fb, fb, over(mx, E3), ALU.mult))
                V.do(dve.tensor_reduce(mx, w, AX.X, ALU.add))
                V.do(dve.tensor_scalar(mn, mx, 1e-8, None, ALU.is_lt))
                V.do(dve.tensor_tensor(fb, fb, w, ALU.subtract))
                V.do(dve.tensor_tensor(fb, fb, over(mn, E3), ALU.mult))
                V.do(dve.tensor_tensor(w, w, fb, ALU.add))
                V.do(dve.tensor_reduce(mx, w, AX.X, ALU.add))
                V.do(dve.tensor_scalar(mx, mx, 1e-8, None, ALU.max))
                V.do(dve.reciprocal(mx, mx))
                V.do(dve.tensor_tensor(w, w, over(mx, E3), ALU.mult))
                split3(w, E3, False)

            layer_norm(5)
            fp8_weights()
            dve.wait_ge(s_in["g3"], 32)
            V.go(dve.tensor_tensor(g3[:, 2:3], g3[:, 0:1], g3[:, 1:2], ALU.mult), s_g3)
            dve.wait_ge(s_g3, 1)
            for n in range(H3 // 2):
                l3_vo_lo(n)
            for c in range(NLC):
                lora(c)
            fp8_quant()
            for b in range(B):
                fp8_out(b)
            layer_norm(6)
            for b in range(B):
                front_lo(6, b, 2 * b)
            for j in range(2):
                l3_make(0, j)
            for kq in range(2):
                l3_sums(0, kq)
            N3 = B * H3
            for n in range(N3 + 6):
                if n > H3 and (n - 6) % H3 == H3 - 1:
                    l3_add((n - 6) // H3)
                if n < N3:
                    l3_scale(n)
                if 4 <= n < N3 + 4:
                    l3_mixed_lo(n - 4)
                if 1 <= n <= N3:
                    l3_normal(n - 1)
                if 2 <= n < N3 + 2:
                    l3_turned_lo(n - 2)
                if n // HG + 1 < NG:
                    l3_make(n // HG + 1, n % HG)
                if n % HG in (1, 2) and n // HG + 1 < NG:
                    l3_sums(n // HG + 1, n % HG - 1)
            layer_norm(7)
            for b in range(B):
                front_lo(7, b, 2 * b)
            router3()
            ffn(1, NJ3)


def _rows(a, n=128):
    return a.reshape(-1, n, a.shape[-1]).transpose(1, 0, 2)


def _layout(np, v):
    f = np.float32
    xs = _rows(v["x"].reshape(B * S, D))
    ident = np.eye(128, dtype=f)
    s0 = np.zeros((3, E0 + 1, F0), f)
    for e in range(E0):
        s0[:, e, e * I0:(e + 1) * I0] = 1
    s0[:, E0, E0 * I0:] = 1
    s3 = np.zeros((3, E3, F3), f)
    for e in range(E3):
        s3[:, e, e * I3:(e + 1) * I3] = 1
    sr = np.zeros((3, HG, HG, 128), f)
    for h in range(HG):
        sr[:, h, h] = 1
    masks = np.zeros((128, 2, 2), f)
    masks[:, :, 0] = 1
    masks[128 - DCA:, 1, 0] = 0
    masks[128 - DCA:, 1, 1] = 1
    gu = v["fside_BxS2xS2_0"].transpose(2, 0, 1)
    gu = gu.reshape(KD, 128, B, D).transpose(1, 2, 0, 3)
    ctx_t = v["ctx_1024"].transpose(2, 0, 1)
    ctx = v["ctx_1024"].reshape(B, 2, 128, C).transpose(2, 0, 1, 3)

    def cols(w):
        return w.reshape(KD, 128, -1).transpose(1, 0, 2)

    def ffn(g, u, d):
        n = g.shape[1] // 128
        parts = [w.reshape(KD, 128, n, 128).transpose(1, 2, 0, 3).reshape(128, n, D) for w in (g, u)]
        return np.concatenate(parts + [_rows(d)], axis=2)

    cat = np.concatenate
    wg = cat([v["L0_ffn_wg"].reshape(-1, D), v["L0_ffn_sg"]]).T
    wu = cat([v["L0_ffn_wu"].reshape(-1, D), v["L0_ffn_su"]]).T
    wd = cat([v["L0_ffn_wd"].transpose(0, 2, 1).reshape(-1, D), v["L0_ffn_sd"].T])
    kv = cat([v["L2_xattn_Wk"], v["L2_xattn_Wv"]], axis=1).reshape(C, H2, 2, HD2).transpose(0, 2, 1, 3)
    bkv = cat([v["L2_xattn_bk"], v["L2_xattn_bv"]]).reshape(H2, 2, HD2).transpose(1, 0, 2)
    g3 = v["L3_ffn_Wg"].transpose(1, 0, 2).reshape(D, F3)
    u3 = v["L3_ffn_Wu"].transpose(1, 0, 2).reshape(D, F3)
    d3 = v["L3_ffn_Wd"].reshape(F3, D)
    aff = cat([v[f"L2_xattn_{n}"] for n in ("bq", "bo", "qn_w", "qn_b", "kn_w", "kn_b", "kn_dca_w", "kn_dca_b")]
              + [bkv.reshape(-1), v["L2_xattn_bkv_dca"]])
    return {
        "x": xs, "ident": ident, "sel0": s0.reshape(K0, F0), "sel3": s3.reshape(K3, F3),
        "selr": sr.reshape(3 * HG, -1), "masks": masks,
        "iota": np.arange(16, dtype=f), "gu_t": gu, "ctx_t": ctx_t, "ctx": ctx,
        "w_rt": cat([cols(v["L0_ffn_cls_w"].T), cols(v["L0_ffn_gate_w"].T)], axis=2),
        "rt_aff": cat([v["L0_ffn_extra_scale"], v["L0_ffn_extra_bias"]]),
        "w_ffn0": ffn(wg, wu, wd),
        "l1_w": cat([v["L1_xattn_Wq"].T, v["L1_xattn_Wk"].T], axis=1),
        "l1_b": np.stack([v["L1_xattn_bq"], v["L1_xattn_bk"]], axis=1),
        "w_up": cols(v["L1_ffn_w_up"].T), "w_dn": _rows(v["L1_ffn_w_down"].T),
        "l2_q": cols(v["L2_xattn_Wq"]), "l2_kv": kv.reshape(C, 2 * D), "l2_dca": v["L2_xattn_Wkv_dca"],
        "l2_o": _rows(v["L2_xattn_Wo"]), "l2_aff": aff,
        "w8": v["L2_ffn_weight"].view(np.uint8).T.reshape(KD, 128, D).transpose(1, 0, 2),
        "w8_sc": v["L2_ffn_weight_scale"].reshape(1), "in_sc": v["L2_ffn_input_scale"].reshape(1),
        "l3_q": cols(v["L3_xattn_Wq"]), "l3_k": v["L3_xattn_Wk"],
        "l3_v": v["L3_xattn_Wv"].reshape(C, H3, HD3).transpose(2, 1, 0),
        "l3_o": _rows(v["L3_xattn_Wo"]),
        "l3_g": np.stack([v["L3_xattn_gq"], v["L3_xattn_gk"]], axis=1),
        "w_ffn3": ffn(g3, u3, d3),
        "lo_a": np.stack([v["L3_ffn_Ga"], v["L3_ffn_Ua"]], axis=1).transpose(3, 0, 1, 2),
        "lo_b": np.stack([v["L3_ffn_Gb"], v["L3_ffn_Ub"]], axis=1).transpose(2, 0, 1, 3),
        "lo_da": v["L3_ffn_Da"].transpose(2, 0, 1), "lo_db": v["L3_ffn_Db"].transpose(1, 0, 2),
        "w_r3": cols(v["L3_ffn_Wr"]), "temp": v["L3_ffn_temperature"],
    }


def kernel(**inputs):
    import numpy as np
    import concourse.bacc as bacc
    from concourse.bass_utils import run_bass_kernel_spmd

    nc = bacc.Bacc("TRN2", target_bir_lowering=False, num_devices=1)
    arrays, args = {}, []
    for name, a in _layout(np, inputs).items():
        a = np.ascontiguousarray(a)
        arrays[f"in_{name}"] = a
        args.append(nc.dram_tensor(f"in_{name}", a.shape, mybir.dt.from_np(a.dtype), kind="ExternalInput").ap())
    args.append(nc.dram_tensor("out_0", (128, NT, D), mybir.dt.float32, kind="ExternalOutput").ap())
    program(nc, *args)
    r = run_bass_kernel_spmd(nc, [arrays], core_ids=[0])
    return r.results[0]["out_0"].transpose(1, 0, 2).reshape(B, S, D)
```
